# Optimizing a Trainium2 kernel written in Bass

```python
import numpy as np
import jax
import jax.numpy as jnp

def _softmax(x, axis=-1):
    return jax.nn.softmax(x, axis=axis)

def _gelu(x):
    return jax.nn.gelu(x, approximate=True)

def _silu(x):
    return jax.nn.silu(x)

def _sigmoid(x):
    return jax.nn.sigmoid(x)

def _layernorm(x, axis=-1, eps=1e-05):
    m = jnp.mean(x, axis=axis, keepdims=True)
    v = jnp.var(x, axis=axis, keepdims=True)
    return (x - m) / jnp.sqrt(v + eps)

def _scatter_add(tgt, idx, src, axis=0):
    return tgt.at[idx].add(src)

def _segment_sum(src, seg, n):
    return jax.ops.segment_sum(src, seg, n)
kernel_name = 'mk_adj_preln_d4_adj_r2_e6c858'

def setup_inputs(seed: int=0):
    np.random.seed(seed)
    _w = jnp.asarray

    def _rec_inputs():
        import jax
        import jax.numpy as jnp
        _gk = jax.random.key(seed)
        x = -0.000929 + 1 * jax.random.normal(jax.random.fold_in(_gk, 1), (4096, 128), jnp.float32)
        _w = (1.0 + jnp.arange(4096, dtype=jnp.float32)) ** (-0.5)
        _w = _w / _w.mean()
        _pij = jnp.clip(0.000488281 * _w[:, None] * _w[None, :], 0.0, 1.0)
        _a = jax.random.uniform(jax.random.fold_in(_gk, 2), (4096, 4096)) < _pij
        _a = jnp.logical_or(_a, jnp.eye(4096, dtype=bool))
        _af = _a.astype(jnp.float32)
        _af = _af * jax.random.uniform(jax.random.fold_in(_gk, 3), (4096, 4096), jnp.float32, 0.05, 1)
        adj = _af
        return (x, adj)
    x, adj = _rec_inputs()

    def _L0_gnn_setup():
        import jax, jax.numpy as jnp
        import numpy as np
        N, E, D = (4096, 4096, 128)
        key = jax.random.key(seed)
        k1, k2 = jax.random.split(key)
        X = jax.random.normal(k1, (N, D), dtype=jnp.float32)
        H = jax.random.uniform(k2, (N, E), dtype=jnp.float32)
        return {'X': X, 'H': H}
    _L0_gnn_all = _L0_gnn_setup()
    _L0_gnn_in = {k: v for k, v in _L0_gnn_all.items() if k in ()}
    del _L0_gnn_all

    def _L1_gnn_setup():
        import jax, jax.numpy as jnp
        import numpy as np
        N, IN, H, C = (2048, 128, 4, 32)
        HC = H * C
        EDGE_P = 0.008

        def _linear_params(key, fan_in, fan_out, bias=True):
            k1, k2 = jax.random.split(key)
            lim = 1.0 / np.sqrt(fan_in)
            W = jax.random.uniform(k1, (fan_in, fan_out), jnp.float32, -lim, lim)
            if not bias:
                return W
            b = jax.random.uniform(k2, (fan_out,), jnp.float32, -lim, lim)
            return (W, b)

        def _transformer_conv(x, adj, Wq, bq, Wk, bk, Wv, bv, Ws, bs, Wb):
            n = x.shape[0]
            q = (x @ Wq + bq).reshape(n, H, C)
            k = (x @ Wk + bk).reshape(n, H, C)
            v = (x @ Wv + bv).reshape(n, H, C)
            attn = jnp.einsum('nhc,mhc->hnm', q, k) / np.float32(np.sqrt(C))
            mask = adj == 0.0
            neg = jnp.where(mask[None], -jnp.inf, attn)
            m = jnp.max(neg, axis=-1, keepdims=True)
            all_inf = jnp.isneginf(m)
            e = jnp.where(mask[None], 0.0, jnp.exp(neg - jnp.where(all_inf, 0.0, m)))
            denom = jnp.sum(e, axis=-1, keepdims=True)
            alpha = e / jnp.where(denom == 0.0, 1.0, denom)
            out = jnp.einsum('hnm,mhc->hnc', alpha, v)
            out = jnp.transpose(out, (1, 2, 0)).reshape(n, C * H)
            x_r = x @ Ws + bs
            beta = jax.nn.sigmoid(jnp.concatenate([out, x_r, out - x_r], axis=-1) @ Wb)
            return beta * x_r + (1.0 - beta) * out
        key = jax.random.key(seed)
        ks = jax.random.split(key, 7)
        x = jax.random.normal(ks[0], (N, IN), jnp.float32)
        adj = (jax.random.uniform(ks[1], (N, N)) < EDGE_P).astype(jnp.float32)
        Wq, bq = _linear_params(ks[2], IN, HC)
        Wk, bk = _linear_params(ks[3], IN, HC)
        Wv, bv = _linear_params(ks[4], IN, HC)
        Ws, bs = _linear_params(ks[5], IN, HC)
        Wb = _linear_params(ks[6], 3 * HC, 1, bias=False)
        return dict(x=x, adj=adj, Wq=Wq, bq=bq, Wk=Wk, bk=bk, Wv=Wv, bv=bv, Ws=Ws, bs=bs, Wb=Wb)
    _L1_gnn_all = _L1_gnn_setup()
    _L1_gnn_in = {k: v for k, v in _L1_gnn_all.items() if k in ('Wq', 'bq', 'Wk', 'bk', 'Wv', 'bv', 'Ws', 'bs', 'Wb')}
    del _L1_gnn_all

    def _L2_gnn_setup():
        import jax, jax.numpy as jnp
        import numpy as np
        N, DIM = (8192, 128)

        def _gru_cell(x, h, W_ih, W_hh, b_ih, b_hh):
            gi = x @ W_ih.T + b_ih
            gh = h @ W_hh.T + b_hh
            i_r, i_z, i_n = jnp.split(gi, 3, axis=-1)
            h_r, h_z, h_n = jnp.split(gh, 3, axis=-1)
            r = jax.nn.sigmoid(i_r + h_r)
            z = jax.nn.sigmoid(i_z + h_z)
            n = jnp.tanh(i_n + r * h_n)
            return (1.0 - z) * n + z * h
        key = jax.random.key(seed)
        ks = jax.random.split(key, 8)
        states = jax.random.normal(ks[0], (N, DIM), dtype=jnp.float32)
        adj = jax.random.uniform(ks[1], (N, N), dtype=jnp.float32)
        s = 1.0 / np.sqrt(DIM)
        W_msg = jax.random.uniform(ks[2], (DIM, DIM), minval=-s, maxval=s, dtype=jnp.float32)
        b_msg = jax.random.uniform(ks[3], (DIM,), minval=-s, maxval=s, dtype=jnp.float32)
        W_ih = jax.random.uniform(ks[4], (3 * DIM, DIM), minval=-s, maxval=s, dtype=jnp.float32)
        W_hh = jax.random.uniform(ks[5], (3 * DIM, DIM), minval=-s, maxval=s, dtype=jnp.float32)
        b_ih = jax.random.uniform(ks[6], (3 * DIM,), minval=-s, maxval=s, dtype=jnp.float32)
        b_hh = jax.random.uniform(ks[7], (3 * DIM,), minval=-s, maxval=s, dtype=jnp.float32)
        return {'states': states, 'adj': adj, 'W_msg': W_msg, 'b_msg': b_msg, 'W_ih': W_ih, 'W_hh': W_hh, 'b_ih': b_ih, 'b_hh': b_hh}
    _L2_gnn_all = _L2_gnn_setup()
    _L2_gnn_in = {k: v for k, v in _L2_gnn_all.items() if k in ('W_msg', 'b_msg', 'W_ih', 'W_hh', 'b_ih', 'b_hh')}
    del _L2_gnn_all

    def _L3_gnn_setup():
        import jax, jax.numpy as jnp
        import numpy as np
        N = 8192
        IN_DIM = 128
        OUT_DIM = 128

        def _message(X, A, W):
            deg = jnp.sum(A, axis=1, keepdims=True)
            A_norm = A / jnp.where(deg > 0, deg, 1.0)
            return A_norm @ X @ W
        key = jax.random.key(seed)
        k1, k2, k3, k4 = jax.random.split(key, 4)
        X = jax.random.normal(k1, (N, IN_DIM), dtype=jnp.float32)
        A = jax.random.uniform(k2, (N, N), dtype=jnp.float32)
        W_in = jax.random.normal(k3, (IN_DIM, OUT_DIM), dtype=jnp.float32) / np.sqrt(IN_DIM)
        W_out = jax.random.normal(k4, (IN_DIM, OUT_DIM), dtype=jnp.float32) / np.sqrt(IN_DIM)
        return {'X': X, 'A': A, 'W_in': W_in, 'W_out': W_out}
    _L3_gnn_all = _L3_gnn_setup()
    _L3_gnn_in = {k: v for k, v in _L3_gnn_all.items() if k in ('W_in', 'W_out')}
    del _L3_gnn_all
    return {'x': x, 'adj': adj, 'L1_gnn_Wq': _L1_gnn_in['Wq'], 'L1_gnn_bq': _L1_gnn_in['bq'], 'L1_gnn_Wk': _L1_gnn_in['Wk'], 'L1_gnn_bk': _L1_gnn_in['bk'], 'L1_gnn_Wv': _L1_gnn_in['Wv'], 'L1_gnn_bv': _L1_gnn_in['bv'], 'L1_gnn_Ws': _L1_gnn_in['Ws'], 'L1_gnn_bs': _L1_gnn_in['bs'], 'L1_gnn_Wb': _L1_gnn_in['Wb'], 'L2_gnn_W_msg': _L2_gnn_in['W_msg'], 'L2_gnn_b_msg': _L2_gnn_in['b_msg'], 'L2_gnn_W_ih': _L2_gnn_in['W_ih'], 'L2_gnn_W_hh': _L2_gnn_in['W_hh'], 'L2_gnn_b_ih': _L2_gnn_in['b_ih'], 'L2_gnn_b_hh': _L2_gnn_in['b_hh'], 'L3_gnn_W_in': _L3_gnn_in['W_in'], 'L3_gnn_W_out': _L3_gnn_in['W_out']}

def reference(x, adj, L1_gnn_Wq, L1_gnn_bq, L1_gnn_Wk, L1_gnn_bk, L1_gnn_Wv, L1_gnn_bv, L1_gnn_Ws, L1_gnn_bs, L1_gnn_Wb, L2_gnn_W_msg, L2_gnn_b_msg, L2_gnn_W_ih, L2_gnn_W_hh, L2_gnn_b_ih, L2_gnn_b_hh, L3_gnn_W_in, L3_gnn_W_out):
    import jax
    import jax.numpy as jnp

    def _L0_gnn_ref(X, H):
        import jax, jax.numpy as jnp
        import numpy as np
        N, E, D = (4096, 4096, 128)
        msg = jnp.matmul(H.T, X)
        inv_deg = 1.0 / H.sum(axis=0)
        inv_deg = jnp.where(jnp.isinf(inv_deg), 0.0, inv_deg)
        return msg * inv_deg[:, None]

    def _L1_gnn_ref(x, adj, Wq, bq, Wk, bk, Wv, bv, Ws, bs, Wb):
        import jax, jax.numpy as jnp
        import numpy as np
        N, IN, H, C = (2048, 128, 4, 32)
        HC = H * C
        EDGE_P = 0.008

        def _linear_params(key, fan_in, fan_out, bias=True):
            k1, k2 = jax.random.split(key)
            lim = 1.0 / np.sqrt(fan_in)
            W = jax.random.uniform(k1, (fan_in, fan_out), jnp.float32, -lim, lim)
            if not bias:
                return W
            b = jax.random.uniform(k2, (fan_out,), jnp.float32, -lim, lim)
            return (W, b)

        def _transformer_conv(x, adj, Wq, bq, Wk, bk, Wv, bv, Ws, bs, Wb):
            n = x.shape[0]
            q = (x @ Wq + bq).reshape(n, H, C)
            k = (x @ Wk + bk).reshape(n, H, C)
            v = (x @ Wv + bv).reshape(n, H, C)
            attn = jnp.einsum('nhc,mhc->hnm', q, k) / np.float32(np.sqrt(C))
            mask = adj == 0.0
            neg = jnp.where(mask[None], -jnp.inf, attn)
            m = jnp.max(neg, axis=-1, keepdims=True)
            all_inf = jnp.isneginf(m)
            e = jnp.where(mask[None], 0.0, jnp.exp(neg - jnp.where(all_inf, 0.0, m)))
            denom = jnp.sum(e, axis=-1, keepdims=True)
            alpha = e / jnp.where(denom == 0.0, 1.0, denom)
            out = jnp.einsum('hnm,mhc->hnc', alpha, v)
            out = jnp.transpose(out, (1, 2, 0)).reshape(n, C * H)
            x_r = x @ Ws + bs
            beta = jax.nn.sigmoid(jnp.concatenate([out, x_r, out - x_r], axis=-1) @ Wb)
            return beta * x_r + (1.0 - beta) * out
        return _transformer_conv(x, adj, Wq, bq, Wk, bk, Wv, bv, Ws, bs, Wb)

    def _L2_gnn_ref(states, adj, W_msg, b_msg, W_ih, W_hh, b_ih, b_hh):
        import jax, jax.numpy as jnp
        import numpy as np
        N, DIM = (8192, 128)

        def _gru_cell(x, h, W_ih, W_hh, b_ih, b_hh):
            gi = x @ W_ih.T + b_ih
            gh = h @ W_hh.T + b_hh
            i_r, i_z, i_n = jnp.split(gi, 3, axis=-1)
            h_r, h_z, h_n = jnp.split(gh, 3, axis=-1)
            r = jax.nn.sigmoid(i_r + h_r)
            z = jax.nn.sigmoid(i_z + h_z)
            n = jnp.tanh(i_n + r * h_n)
            return (1.0 - z) * n + z * h
        agg = adj @ states
        msg = jax.nn.relu(agg @ W_msg.T + b_msg)
        return _gru_cell(msg, states, W_ih, W_hh, b_ih, b_hh)

    def _L3_gnn_ref(X, A, W_in, W_out):
        import jax, jax.numpy as jnp
        import numpy as np
        N = 8192
        IN_DIM = 128
        OUT_DIM = 128

        def _message(X, A, W):
            deg = jnp.sum(A, axis=1, keepdims=True)
            A_norm = A / jnp.where(deg > 0, deg, 1.0)
            return A_norm @ X @ W
        X_in = _message(X, A, W_in)
        X_out = _message(X, A.T, W_out)
        return X_in + X_out
    h = jnp.maximum(_layernorm(x, axis=-1), 0.0)
    x = x + _L0_gnn_ref(h, adj)
    h = jnp.maximum(_layernorm(x, axis=-1), 0.0)
    x = x + _L1_gnn_ref(h, adj, L1_gnn_Wq, L1_gnn_bq, L1_gnn_Wk, L1_gnn_bk, L1_gnn_Wv, L1_gnn_bv, L1_gnn_Ws, L1_gnn_bs, L1_gnn_Wb)
    h = jnp.maximum(_layernorm(x, axis=-1), 0.0)
    x = x + _L2_gnn_ref(h, adj, L2_gnn_W_msg, L2_gnn_b_msg, L2_gnn_W_ih, L2_gnn_W_hh, L2_gnn_b_ih, L2_gnn_b_hh)
    h = jnp.maximum(_layernorm(x, axis=-1), 0.0)
    x = x + _L3_gnn_ref(h, adj, L3_gnn_W_in, L3_gnn_W_out)
    return x

_drawn_inputs = setup_inputs


def setup_inputs(seed=0):
    import zlib

    import numpy as np

    out = dict(_drawn_inputs(seed))
    spreads = {}
    factors = {'L1_gnn_Wq': 8.0,
     'L1_gnn_bq': 24.951,
     'L1_gnn_Wk': 8.0,
     'L1_gnn_bk': 64.0,
     'L1_gnn_bv': 3.131,
     'L1_gnn_bs': 2.777,
     'L2_gnn_b_msg': 8.0,
     'L2_gnn_b_ih': 3.714,
     'L2_gnn_b_hh': 6.434}
    for name, (base, spread) in spreads.items():
        noise = np.random.default_rng([zlib.crc32(name.encode()), seed]).standard_normal(out[name].shape)
        drawn = base * np.exp(spread * noise) if base else spread * noise
        out[name] = jnp.asarray(drawn.astype(out[name].dtype))
    for name, factor in factors.items():
        out[name] = (out[name] * factor).astype(out[name].dtype)
    return out
```

```python
from contextlib import ExitStack

import concourse.bass as bass
from concourse import mybir

P = 128
N = 4096
D = 128
NB = N // P
CW = 512
NCH = N // CW
CB = CW // P
GR = 4
NG = NB // GR
HEADS = 4
HC = D // HEADS
SW = 1024
NS = N // SW
EPS = 1e-5
HIDE = -1.0e30
LOWEST = -3.0e38

F32 = mybir.dt.float32
F32R = mybir.dt.float32r
BF16 = mybir.dt.bfloat16
ALU = mybir.AluOpType
ACT = mybir.ActivationFunctionType
AX_X = mybir.AxisListType.X


class Places:
    pass


class Chain:

    def __init__(self, engine, sem, base=0):
        self.engine, self.sem, self.base, self.n = engine, sem, base, 0

    def __call__(self, instruction):
        self.n += 1
        instruction.then_inc(self.sem, 1)
        self.engine.wait_ge(self.sem, self.base + self.n)


def wait_apart(engine, passed, sem, value):
    engine.wait_ge(sem, value)
    engine.sem_inc(passed, 1)


def over(stat, blocks):
    return stat.unsqueeze(2).to_broadcast([P, blocks, D])


def normalise(step, dve, x, h, centred, square, stat, blocks, var_ready, std_ready, turn):
    total, mean, var, std, inv, tmp = (stat[:, k, :] for k in range(6))
    step(dve.reduce_sum(total, x, AX_X))
    step(dve.tensor_scalar(mean, total, 1.0 / D, None, ALU.mult))
    step(dve.tensor_tensor(centred, x, over(mean, blocks), ALU.subtract))
    step(dve.tensor_tensor(square, centred, centred, ALU.mult))
    step(dve.reduce_sum(total, square, AX_X))
    dve.tensor_scalar(var, total, 1.0 / D, EPS, ALU.mult, ALU.add).then_inc(var_ready, 1)
    dve.wait_ge(std_ready, turn)
    step(dve.reciprocal(inv, std))
    step(dve.tensor_tensor(tmp, inv, inv, ALU.mult))
    step(dve.tensor_tensor(tmp, tmp, var, ALU.mult))
    step(dve.tensor_scalar(tmp, tmp, -0.5, 1.5, ALU.mult, ALU.add))
    step(dve.tensor_tensor(inv, inv, tmp, ALU.mult))
    return dve.scalar_tensor_tensor(h, centred, 0.0, over(inv, blocks), ALU.max, ALU.mult)


NORM_STEPS = 10


def root(act, stat, var_ready, std_ready, turn):
    act.wait_ge(var_ready, turn)
    act.activation(stat[:, 3, :], stat[:, 2, :], ACT.Sqrt).then_inc(std_ready, 1)


def setup(nc, t, m, dram):
    with ExitStack() as ctx:
        sb = lambda name, shape, dt=F32: ctx.enter_context(nc.sbuf_tensor(name, shape, dt))
        sem = lambda name: ctx.enter_context(nc.semaphore(name))
        x = sb("su_x", [P, NB, D])
        centred = sb("su_centred", [P, NB, D])
        square = sb("su_square", [P, NB, D])
        stat = sb("su_stat", [P, 6, NB])
        raw = sb("su_raw", [P, 7, D])
        turned = ctx.enter_context(nc.psum_tensor("su_turned", [P, 8 * P], F32))
        x_loaded, w_loaded, zeroed, ident_ready = (sem(f"su_{n}") for n in ("x_loaded", "w_loaded", "zeroed", "ident_ready"))
        turned_ready, var_ready, std_ready, steps = (sem(f"su_{n}") for n in ("turned_ready", "var_ready", "std_ready", "steps"))
        block = ctx.enter_context(nc.Block())
        one_col = lambda v: v.rearrange("(p a) -> p a", a=1)
        weights = [
            (raw[:, 0, :], t["L2_gnn_W_msg"]),
            (raw[:, 1:4, :], t["L2_gnn_W_ih"].rearrange("(g o) d -> o g d", g=3)),
            (raw[:, 4:7, :], t["L2_gnn_W_hh"].rearrange("(g o) d -> o g d", g=3)),
            (m.w_q[:], t["L1_gnn_Wq"]), (m.w_k[:], t["L1_gnn_Wk"]),
            (m.w_vs[:, 0:D], t["L1_gnn_Wv"]), (m.w_vs[:, D:2 * D], t["L1_gnn_Ws"]),
            (m.w_io[:, 0:D], t["L3_gnn_W_in"]), (m.w_io[:, D:2 * D], t["L3_gnn_W_out"]),
            (m.b_q[:], one_col(t["L1_gnn_bq"])), (m.b_k[:], one_col(t["L1_gnn_bk"])),
            (m.b_vs[:, 0:D], t["L1_gnn_bv"].partition_broadcast(P)), (m.b_vs[:, D:2 * D], t["L1_gnn_bs"].partition_broadcast(P)),
            (m.w_beta[:], t["L1_gnn_Wb"].rearrange("n o -> (n o)").partition_broadcast(P)),
            (m.b_msg[:], one_col(t["L2_gnn_b_msg"])),
        ]
        for gate in range(3):
            rows = slice(gate * D, (gate + 1) * D)
            weights += [(m.b_ih[:, gate:gate + 1], one_col(t["L2_gnn_b_ih"][rows])),
                        (m.b_hh[:, gate:gate + 1], one_col(t["L2_gnn_b_hh"][rows]))]

        @block.sync
        def _(sp):
            sp.dma_start(x[:], t["x"].rearrange("(b p) d -> p b d", p=P)).then_inc(x_loaded, 16)
            for to, of in weights:
                sp.dma_start(to, of).then_inc(w_loaded, 16)

        @block.gpsimd
        def _(pool):
            pool.memset(m.ident[:], 0.0).then_inc(zeroed, 1)
            pool.memset(m.ones[:], 1.0)
            pool.wait_ge(zeroed, 1)
            pool.affine_select(out=m.ident[:], in_=m.ident[:], compare_op=ALU.not_equal, fill=1.0, base=0,
                               pattern=[[-1, P]], channel_multiplier=1).then_inc(ident_ready, 1)

        @block.tensor
        def _(pe):
            pe.wait_ge(ident_ready, 1)
            pe.wait_ge(w_loaded, 16 * len(weights))
            for k in range(7):
                last = pe.transpose(turned[:, k * P:(k + 1) * P], raw[:, k, :], m.ident[:])
            last.then_inc(turned_ready, 1)

        @block.scalar
        def _(act):
            root(act, stat, var_ready, std_ready, 1)
            act.wait_ge(turned_ready, 1)
            act.activation(m.w_gru[:], turned[:, 0:7 * P].rearrange("p (k o) -> p k o", k=7), ACT.Copy)

        @block.vector
        def _(dve):
            step = Chain(dve, steps)
            dve.wait_ge(ident_ready, 1)
            step(dve.tensor_tensor(m.ident_sum[:], m.ident[:, 0:HC], m.ident[:, HC:2 * HC], ALU.add))
            step(dve.tensor_tensor(m.ident_sum[:], m.ident_sum[:], m.ident[:, 2 * HC:3 * HC], ALU.add))
            step(dve.tensor_tensor(m.ident_sum[:], m.ident_sum[:], m.ident[:, 3 * HC:4 * HC], ALU.add))
            dve.wait_ge(w_loaded, 16 * len(weights))
            step(dve.tensor_tensor(m.b_rz[:], m.b_ih[:, 0:2], m.b_hh[:, 0:2], ALU.add))
            dve.wait_ge(x_loaded, 16)
            normalise(step, dve, x[:], m.h[:], centred[:], square[:], stat, NB, var_ready, std_ready, 1)


def layer0(nc, t, m, dram):
    RING, STAGES = 4, 2
    with ExitStack() as ctx:
        sb = lambda name, shape, dt=F32: ctx.enter_context(nc.sbuf_tensor(name, shape, dt))
        bank = lambda name, n=1: ctx.enter_context(nc.psum_tensor(name, [P, n * CW], F32))
        sem = lambda name: ctx.enter_context(nc.semaphore("l0_" + name))
        a_in = sb("l0_a_in", [P, RING, GR, CW])
        stage = sb("l0_stage", [P, STAGES, CB, GR * P])
        colsum = sb("l0_colsum", [P, CW])
        part = sb("l0_part", [P, 2, CW])
        msg_t = sb("l0_msg_t", [P, CW])
        x_c = sb("l0_x_c", [P, CB, D])
        h_c = sb("l0_h_c", [P, CB, D])
        centred = sb("l0_centred", [P, CB, D])
        square = sb("l0_square", [P, CB, D])
        h_t = sb("l0_h_t", [P, CW])
        full = sb("l0_full", [P, 2, CW])
        high = sb("l0_high", [P, 2, CW], F32R)
        low = sb("l0_low", [P, 2, CW], F32R)
        skip = sb("l0_skip", [P, CB, D])
        stat = sb("l0_stat", [P, 6, CB])
        deg = sb("l0_deg", [P, 5, CB])
        acc = bank("l0_acc")
        turned = [bank(f"l0_turned{b}") for b in range(CB)]
        node = bank("l0_node")
        proj = bank("l0_proj", 2)
        loaded = [sem(f"loaded{s}") for s in range(RING)]
        stored = [sem(f"stored{s}") for s in range(STAGES)]
        (summed, block_turned, block_staged, acc_ready, colsum_ready, deg_ready, msg_out, msg_turned, x_loaded,
         x1_ready, x1_stored, var_ready, std_ready, h_ready, h_turned, ht_ready, qk_ready, qk_split, qk_stored,
         k_stored, k_loaded, vs_ready, vs_out, skip_stored, steps, sum_steps) = (sem(n) for n in (
             "summed", "block_turned", "block_staged", "acc_ready", "colsum_ready", "deg_ready", "msg_out",
             "msg_turned", "x_loaded", "x1_ready", "x1_stored", "var_ready", "std_ready", "h_ready", "h_turned",
             "ht_ready", "qk_ready", "qk_split", "qk_stored", "k_stored", "k_loaded", "vs_ready", "vs_out",
             "skip_stored", "steps", "sum_steps"))
        STEPS = 4 + 3 + NORM_STEPS
        block = ctx.enter_context(nc.Block())
        a_rows = t["adj"].rearrange("(g r p) n -> g p r n", r=GR, p=P)
        at_rows = dram.adj_t.rearrange("(c b p) m -> c p b m", b=CB, p=P)
        nodes = lambda v: v.rearrange("(c b p) d -> c p b d", b=CB, p=P)

        def each(engine, body):
            body(0, None, True)
            body(1, 0, False)
            with engine.Fori(2, NCH) as c:
                body(c, c - 1, False)
            body(None, NCH - 1, False)

        @block.sync
        def _(sp):
            def store(c, g):
                wait_apart(sp, m.passed, block_staged, CB * (NG * c + g) + CB)
                sp.dma_start(at_rows[c, :, :, g * GR * P:(g + 1) * GR * P] if isinstance(c, int) else
                             at_rows[bass.ts(c, 1), :, :, g * GR * P:(g + 1) * GR * P].squeeze(0),
                             stage[:, g % STAGES]).then_inc(stored[g % STAGES], 16)

            def body(c, e, first):
                if c is None:
                    for g in range(RING, NG):
                        store(NCH - 1, g)
                    for s in stored:
                        sp.wait_ge(s, 16 * NCH * NG // STAGES)
                    return
                for g in range(NG):
                    if not (first and g < RING):
                        wait_apart(sp, m.passed, block_turned, CB * (NG * c + g - RING) + CB)
                        wait_apart(sp, m.passed, summed, NG * c + g - RING + 1)
                    sp.dma_start(a_in[:, g % RING], a_rows[g, :, :, bass.ts(c, CW)]).then_inc(loaded[g % RING], 16)
                    if g >= RING:
                        store(c, g - RING)
                    elif not first:
                        store(c - 1, g + NG - RING)

            each(sp, body)

        @block.tensor
        def _(pe):
            def stream(c, g, first):
                pe.wait_ge(loaded[g % RING], 16 * (NG // RING) * c + 16 * (g // RING) + 16)
                if g == 0 and not first:
                    pe.wait_ge(msg_out, c)
                for r in range(GR):
                    last = pe.matmul(acc[:], m.h[:, GR * g + r, :], a_in[:, g % RING, r, :],
                                     start=(g == 0 and r == 0), stop=(g == NG - 1 and r == GR - 1))
                if g == NG - 1:
                    last.then_inc(acc_ready, 1)
                for b in range(CB):
                    if not (first and g == 0):
                        pe.wait_ge(block_staged, CB * (NG * c + g - 1) + b + 1)
                    for r in range(GR):
                        last = pe.transpose(turned[b][:, r * P:(r + 1) * P], a_in[:, g % RING, r, b * P:(b + 1) * P],
                                            m.ident[:])
                    last.then_inc(block_turned, 1)

            def degrees_and_message(e):
                pe.wait_ge(colsum_ready, e + 1)
                if not (isinstance(e, int) and e == 0):
                    pe.wait_ge(vs_out, e)
                for b in range(CB):
                    last = pe.matmul(proj[:, b:b + 1], colsum[:, b * P:(b + 1) * P], m.ones[:, 0:1], start=True, stop=True)
                last.then_inc(deg_ready, 1)
                pe.wait_ge(msg_out, e + 1)
                for b in range(CB):
                    last = pe.transpose(node[:, b * P:(b + 1) * P], msg_t[:, b * P:(b + 1) * P], m.ident[:])
                last.then_inc(msg_turned, 1)

            def turn_h(e):
                pe.wait_ge(h_ready, e + 1)
                for b in range(CB):
                    last = pe.transpose(node[:, b * P:(b + 1) * P], h_c[:, b, :], m.ident[:])
                last.then_inc(h_turned, 1)

            def project_qk(e):
                pe.wait_ge(ht_ready, e + 1)
                pe.matmul(proj[:, 0:CW], m.w_q[:], h_t[:], start=True, stop=True).then_inc(qk_ready, 1)
                pe.matmul(proj[:, CW:2 * CW], m.w_k[:], h_t[:], start=True, stop=True).then_inc(qk_ready, 1)

            def project_vs(e):
                pe.wait_ge(qk_split, 2 * e + 2)
                for b in range(CB):
                    last = pe.matmul(proj[:, b * 2 * D:(b + 1) * 2 * D], h_t[:, b * P:(b + 1) * P], m.w_vs[:],
                                     start=True, stop=True)
                last.then_inc(vs_ready, 1)

            def body(c, e, first):
                for g in range(NG):
                    if e is not None:
                        for at, part_of in ((0, degrees_and_message), (3, turn_h), (4, project_qk), (6, project_vs)):
                            if at == g:
                                part_of(e)
                    if c is not None:
                        stream(c, g, first)

            each(pe, body)

        @block.scalar
        def _(act):
            def stream(c, g, first):
                for b in range(CB):
                    act.wait_ge(block_turned, CB * (NG * c + g) + b + 1)
                    if b == 0 and not (first and g < STAGES):
                        act.wait_ge(stored[g % STAGES], 16 * (NG // STAGES) * c + 16 * (g // STAGES))
                    act.activation(stage[:, g % STAGES, b, :], turned[b][:], ACT.Copy).then_inc(block_staged, 1)
                if g == NG - 1:
                    act.wait_ge(acc_ready, c + 1)
                    act.activation(msg_t[:], acc[:], ACT.Copy).then_inc(msg_out, 1)

            def body(c, e, first):
                for g in range(NG):
                    if c is not None:
                        stream(c, g, first)
                    if e is not None and g == 0:
                        root(act, stat, var_ready, std_ready, e + 1)
                    if e is not None and g == 2:
                        act.wait_ge(h_turned, e + 1)
                        act.activation(h_t[:], node[:], ACT.Copy).then_inc(ht_ready, 1)

            each(act, body)

        @block.vector
        def _(dve):
            def stream(c, g, first):
                dve.wait_ge(loaded[g % RING], 16 * (NG // RING) * c + 16 * (g // RING) + 16)
                if g == 0:
                    if not first:
                        dve.wait_ge(deg_ready, c)
                    to = colsum[:]
                else:
                    to = part[:, g % 2, :]
                dve.reduce_sum(to, a_in[:, g % RING].rearrange("p r n -> p n r"), AX_X).then_inc(summed, 1)
                dve.wait_ge(summed, NG * c + g + 1)
                if g:
                    add = dve.tensor_tensor(colsum[:], colsum[:], part[:, g % 2, :], ALU.add)
                    if g == NG - 1:
                        add.then_inc(colsum_ready, 1)

            def add_message(e, step):
                dve.wait_ge(deg_ready, e + 1)
                total, empty, safe, inverse, _spare = (deg[:, k, :] for k in range(5))
                step(dve.tensor_scalar(empty, proj[:, 0:CB], 0.0, None, ALU.is_equal))
                step(dve.tensor_tensor(safe, proj[:, 0:CB], empty, ALU.add))
                step(dve.reciprocal(inverse, safe))
                step(dve.tensor_scalar(empty, empty, -1.0, 1.0, ALU.mult, ALU.add))
                step(dve.tensor_tensor(inverse, inverse, empty, ALU.mult))
                dve.wait_ge(x_loaded, 16 * e + 16)
                dve.wait_ge(msg_turned, e + 1)
                step(dve.tensor_tensor(h_c[:], node[:].rearrange("p (b d) -> p b d", b=CB), over(inverse, CB), ALU.mult))
                dve.tensor_tensor(x_c[:], x_c[:], h_c[:], ALU.add).then_inc(x1_ready, 1)
                dve.wait_ge(x1_ready, e + 1)
                normalise(step, dve, x_c[:], h_c[:], centred[:], square[:], stat, CB, var_ready, std_ready, e + 1)\
                    .then_inc(h_ready, 1)

            def split_qk(e, step, later):
                if later:
                    dve.wait_ge(qk_stored, 128 * e)
                for k in range(2):
                    dve.wait_ge(qk_ready, 2 * e + k + 1)
                    if k == 0:
                        step(dve.tensor_scalar(full[:, 0, :], proj[:, 0:CW], m.b_q[:], float(HC) ** -0.5, ALU.add, ALU.mult))
                    else:
                        step(dve.tensor_scalar(full[:, 1, :], proj[:, CW:2 * CW], m.b_k[:], None, ALU.add))
                    step(dve.tensor_copy(high[:, k, :], full[:, k, :]))
                    dve.tensor_tensor(low[:, k, :], full[:, k, :], high[:, k, :].bitcast(F32), ALU.subtract).then_inc(qk_split, 1)

            def add_vs(e, later):
                dve.wait_ge(vs_ready, e + 1)
                if later:
                    dve.wait_ge(skip_stored, 16 * e)
                vs = proj[:].rearrange("p (b k d) -> p b k d", b=CB, k=2)
                bias = lambda k: m.b_vs[:, k * D:(k + 1) * D].unsqueeze(1).to_broadcast([P, CB, D])
                dve.tensor_tensor(m.v[:, bass.ts(e, CB), :], vs[:, :, 0, :], bias(0), ALU.add)
                dve.tensor_tensor(skip[:], vs[:, :, 1, :], bias(1), ALU.add).then_inc(vs_out, 1)

            K_STEPS = 6 + NORM_STEPS + 4

            def body(c, e, first):
                step = None if e is None else Chain(dve, steps, K_STEPS * e)
                later = e is not None and not (isinstance(e, int) and e == 0)
                for g in range(NG):
                    if c is not None:
                        stream(c, g, first)
                    if e is not None and g == 0:
                        add_message(e, step)
                    if e is not None and g == 4:
                        split_qk(e, step, later)
                    if e is not None and g == 6:
                        add_vs(e, later)
                assert e is None or step.n == K_STEPS

            each(dve, body)

        @block.gpsimd
        def _(pool):
            def at(v, c):
                return v[c] if isinstance(c, int) else v[bass.ts(c, 1)].squeeze(0)

            def load_x(c):
                pool.dma_start(x_c[:], at(nodes(t["x"]), c)).then_inc(x_loaded, 16)

            def body(c, e, first):
                if e is None:
                    load_x(0)
                    return
                wait_apart(pool, m.passed, x1_ready, e + 1)
                pool.dma_start(at(nodes(dram.x1), e), x_c[:]).then_inc(x1_stored, 16)
                for k, stack, order in ((0, dram.q_stack, (high, high, low, low)), (1, dram.k_stack, (high, low, high, low))):
                    wait_apart(pool, m.passed, qk_split, 2 * e + k + 1)
                    for s, half in enumerate(order):
                        to = stack[:, s * HC:(s + 1) * HC, bass.ts(e, CW)]
                        pool.dma_start(to, half[:, k, :].bitcast(F32)).then_inc(qk_stored, 16)
                wait_apart(pool, m.passed, vs_out, e + 1)
                pool.dma_start(at(nodes(dram.skip), e), skip[:]).then_inc(skip_stored, 16)
                wait_apart(pool, m.passed, qk_stored, 128 * e + 128)
                pool.dma_start(m.k_stack[:, :, bass.ts(e, CW)].bitcast(F32), dram.k_stack[:, :, bass.ts(e, CW)].rearrange("h s n -> s h n"))\
                    .then_inc(k_loaded, 16)
                wait_apart(pool, m.passed, h_ready, e + 1)
                wait_apart(pool, m.passed, x1_stored, 16 * e + 16)
                if c is not None:
                    load_x(e + 1)
                else:
                    pool.wait_ge(skip_stored, 16 * NCH)
                    pool.wait_ge(k_loaded, 16 * NCH)

            each(pool, body)


def attention(nc, t, m, dram):
    UNITS = HEADS * NB
    LEAD = 2
    GC = 4
    G = NB // GC
    BY_DVE = (3, 7)
    with ExitStack() as ctx:
        sb = lambda name, shape, dt=F32: ctx.enter_context(nc.sbuf_tensor("at_" + name, shape, dt))
        bank = lambda name, n=1: ctx.enter_context(nc.psum_tensor("at_" + name, [P, n * CW], F32))
        sem = lambda name: ctx.enter_context(nc.semaphore("at_" + name))
        a_in = sb("a_in", [P, N])
        mask = sb("mask", [P, 2, N], BF16)
        q_in = sb("q_in", [P, HEADS, P], F32R)
        probs = sb("probs", [P, HEADS, N])
        probs_t = sb("probs_t", [P, G, GC * P])
        top = sb("top", [P, HEADS, NS])
        neg = sb("neg", [P, 2, HEADS])
        sums = sb("sums", [P, HEADS, NS])
        total = sb("total", [P, 3])
        tiles = sb("tiles", [P, 2, P])
        result = sb("result", [P, 2, HC, HEADS])
        scores = [bank(f"scores{k}", 2) for k in range(2)]
        turned = [bank(f"turned{k}") for k in range(2)]
        value = [bank(f"value{k}") for k in range(2)]
        a_loaded = [sem(f"a_loaded{c}") for c in range(NS)]
        q_loaded = [sem(f"q_loaded{h}") for h in range(HEADS)]
        (mask_ready, scores_ready, masked, max_ready, bias_ready, exp_ready, transposed, act_copied, dve_copied,
         tiled, tiles_out, summed, out_ready, steps) = (sem(n) for n in (
             "mask_ready", "scores_ready", "masked", "max_ready", "bias_ready", "exp_ready", "transposed",
             "act_copied", "dve_copied", "tiled", "tiles_out", "summed", "out_ready", "steps"))
        stored = [sem(f"stored{k}") for k in range(2)]
        block = ctx.enter_context(nc.Block())
        a_rows = t["adj"].rearrange("(b p) n -> b p n", p=P)
        out_rows = dram.attended.rearrange("(b p) d -> b p d", p=P)
        row = lambda v, i: v[i] if isinstance(i, int) else v[bass.ts(i, 1)].squeeze(0)

        def wait_copied(engine, u, g):
            if g < 0:
                u, g = u - 1, g + G
            mine = sum(k <= g for k in BY_DVE)
            if g in BY_DVE:
                engine.wait_ge(dve_copied, len(BY_DVE) * u + mine)
            else:
                engine.wait_ge(act_copied, (G - len(BY_DVE)) * u + g + 1 - mine)

        @block.sync
        def _(sp):
            def load_a(i, first=False):
                for c in range(NS):
                    if not first:
                        wait_apart(sp, m.passed, mask_ready, NS * (i - 1) + c + 1)
                    sp.dma_start(a_in[:, c * SW:(c + 1) * SW], row(a_rows, i)[:, c * SW:(c + 1) * SW])\
                        .then_inc(a_loaded[c], 16)

            def load_q(i, first=False):
                for h in range(HEADS):
                    if not first:
                        wait_apart(sp, m.passed, scores_ready, NS * (HEADS * (i - 1) + h) + NS)
                    sp.dma_start(q_in[:, h, :].bitcast(F32), dram.q_stack[h, :, bass.ts(i, P)]).then_inc(q_loaded[h], 16)

            def store(i, k):
                wait_apart(sp, m.passed, out_ready, HEADS * i + HEADS)
                sp.dma_start(row(out_rows, i), result[:, k].rearrange("p c h -> p (c h)")).then_inc(stored[k], 16)

            load_a(0, True)
            load_q(0, True)
            load_a(1)
            load_q(1)
            load_a(2)
            load_q(2)
            store(0, 0)
            with sp.Fori(1, NB // 2 - 1) as j:
                for k in range(2):
                    i = j * 2 + k
                    load_a(i + 1)
                    load_q(i + 1)
                    store(i - 1, 1 - k)
            load_a(NB - 1)
            load_q(NB - 1)
            for i in range(NB - 3, NB):
                store(i, i % 2)
            for k in range(2):
                sp.wait_ge(stored[k], 16 * (NB // 2))

        @block.gpsimd
        def _(pool):
            def make(i, k, first=False):
                for c in range(NS):
                    if c == 0 and not first:
                        pool.wait_ge(masked, NS * HEADS * (i - 1))
                    wait_apart(pool, m.passed, a_loaded[c], 16 * i + 16)
                    pool.tensor_scalar(mask[:, k, c * SW:(c + 1) * SW], a_in[:, c * SW:(c + 1) * SW], 0.0, HIDE,
                                       ALU.is_equal, ALU.mult).then_inc(mask_ready, 1)

            make(0, 0, True)
            make(1, 1, True)
            with pool.Fori(1, NB // 2) as j:
                for k in range(2):
                    make(j * 2 + k, k)

        @block.tensor
        def _(pe):
            def score(u, h, i, c, first=False):
                if c == 0:
                    pe.wait_ge(q_loaded[h], 16 * i + 16)
                if not (first and c < 2):
                    pe.wait_ge(masked, NS * u + c - 1)
                for k in range(SW // CW):
                    at = c * SW + k * CW
                    last = pe.matmul(scores[c % 2][:, k * CW:(k + 1) * CW], q_in[:, h, :],
                                     m.k_stack[:, h, at:at + CW], start=True, stop=True)
                last.then_inc(scores_ready, 1)

            def values(u, h, g):
                if g < 0:
                    h, g, u = (h - 1) % HEADS, g + G, u - 1
                for r in range(GC):
                    last = pe.matmul(value[h % 2][r * HC:(r + 1) * HC, 0:P], m.v[:, g * GC + r, h * HC:(h + 1) * HC],
                                     probs_t[:, g, r * P:(r + 1) * P], start=(g == 0), stop=(g == G - 1))
                if g == G - 1:
                    last.then_inc(tiled, 1)

            def add_tiles(u, k):
                pe.wait_ge(tiles_out, u + 1)
                pe.matmul(value[k][:, P:P + HC], tiles[:, k, :], m.ident_sum[:], start=True, stop=True).then_inc(summed, 1)

            def unit(i, h, first=False, last=False):
                u = i * HEADS + h
                ahead = not (last and h >= HEADS - LEAD)
                for c in range(NS):
                    if ahead:
                        score(u + LEAD, (h + LEAD) % HEADS, i + (h + LEAD) // HEADS, c)
                    pe.wait_ge(exp_ready, NS * u + c + 1)
                    for g in (2 * c, 2 * c + 1):
                        begun = not (first and h == 0 and g < 2)
                        if begun:
                            wait_copied(pe, u, g - 2)
                        for r in range(GC):
                            last_t = pe.transpose(turned[g % 2][:, r * P:(r + 1) * P],
                                                  probs[:, h, (g * GC + r) * P:(g * GC + r + 1) * P], m.ident[:])
                        last_t.then_inc(transposed, 1)
                        if begun:
                            if g == 2 and not (first and h < 2):
                                pe.wait_ge(out_ready, u - 1)
                            values(u, h, g - 2)
                        if g == 4 and not (first and h == 0):
                            add_tiles(u - 1, (h - 1) % 2)

            for c in range(NS):
                score(0, 0, 0, c, first=True)
            for c in range(NS):
                score(1, 1, 0, c)
            for h in range(HEADS):
                unit(0, h, first=True)
            with pe.Fori(1, NB - 1) as i:
                for h in range(HEADS):
                    unit(i, h)
            for h in range(HEADS):
                unit(NB - 1, h, last=True)
            for g in (G - 2, G - 1):
                wait_copied(pe, UNITS - 1, g)
                values(UNITS - 1, HEADS - 1, g)
            add_tiles(UNITS - 1, 1)

        @block.scalar
        def _(act):
            def exponentials(u, h, c):
                if c == 0:
                    act.wait_ge(bias_ready, u + 1)
                act.activation(probs[:, h, c * SW:(c + 1) * SW], probs[:, h, c * SW:(c + 1) * SW], ACT.Exp,
                               bias=neg[:, 1, h:h + 1], accum_out=sums[:, h, c:c + 1]).then_inc(exp_ready, 1)

            def tiles_of(u, k):
                act.wait_ge(tiled, u + 1)
                act.activation(tiles[:, k, :], value[k][:, 0:P], ACT.Copy).then_inc(tiles_out, 1)

            def unit(i, h, first=False, last=False):
                u = i * HEADS + h
                for c in range(NS):
                    if not (last and h == HEADS - 1):
                        exponentials(u + 1, (h + 1) % HEADS, c)
                    for g in (2 * c, 2 * c + 1):
                        if g not in BY_DVE:
                            act.wait_ge(transposed, G * u + g + 1)
                            act.activation(probs_t[:, g, :], turned[g % 2][:], ACT.Copy).then_inc(act_copied, 1)
                        if g == 2 and not (first and h == 0):
                            tiles_of(u - 1, (h - 1) % 2)

            for c in range(NS):
                exponentials(0, 0, c)
            for h in range(HEADS):
                unit(0, h, first=True)
            with act.Fori(1, NB - 1) as i:
                for h in range(HEADS):
                    unit(i, h)
            for h in range(HEADS):
                unit(NB - 1, h, last=True)
            tiles_of(UNITS - 1, 1)

        @block.vector
        def _(dve):
            def mask_part(u, h, i, k, c):
                if h == 0:
                    dve.wait_ge(mask_ready, NS * i + c + 1)
                wait_apart(dve, m.passed, scores_ready, NS * u + c + 1)
                dve.tensor_tensor_reduce(
                    out=probs[:, h, c * SW:(c + 1) * SW], in0=scores[c % 2][:], in1=mask[:, k, c * SW:(c + 1) * SW],
                    scale=1.0, scalar=LOWEST, op0=ALU.add, op1=ALU.max, accum_out=top[:, h, c:c + 1]).then_inc(masked, 1)

            def maximum(u, h):
                dve.wait_ge(masked, NS * u + NS)
                dve.tensor_reduce(neg[:, 0, h:h + 1], top[:, h, :], AX_X, ALU.max, negate=True).then_inc(max_ready, 1)
                dve.wait_ge(max_ready, u + 1)
                dve.scalar_tensor_tensor(neg[:, 1, h:h + 1], neg[:, 0, h:h + 1], -HIDE / 2, neg[:, 0, h:h + 1],
                                         ALU.is_lt, ALU.mult).then_inc(bias_ready, 1)

            def copy_out(u, g):
                dve.wait_ge(transposed, G * u + g + 1)
                dve.tensor_copy(probs_t[:, g, :], turned[g % 2][:]).then_inc(dve_copied, 1)

            def head_out(u, h, i, k, fresh):
                step = Chain(dve, steps, 3 * u)
                dve.wait_ge(exp_ready, NS * u + NS)
                step(dve.reduce_sum(total[:, 0:1], sums[:, h, :], AX_X))
                step(dve.scalar_tensor_tensor(total[:, 1:2], total[:, 0:1], 0.0, total[:, 0:1], ALU.is_equal, ALU.add))
                step(dve.reciprocal(total[:, 2:3], total[:, 1:2]))
                dve.wait_ge(summed, u + 1)
                if h == 0 and not fresh:
                    dve.wait_ge(stored[k], 8 * i - 8 * k)
                dve.tensor_scalar(result[:, k, :, h], value[h % 2][:, P:P + HC], total[:, 2:3], None, ALU.mult)\
                    .then_inc(out_ready, 1)

            def unit(i, h, k, first=False, last=False):
                u = i * HEADS + h
                after = h + LEAD
                for c in range(NS):
                    if not (last and after >= HEADS):
                        mask_part(u + LEAD, after % HEADS, i + after // HEADS, (k + after // HEADS) % 2, c)
                        if c == NS - 1:
                            maximum(u + LEAD, after % HEADS)
                    for g in (2 * c, 2 * c + 1):
                        if g in BY_DVE:
                            copy_out(u, g)
                    if c == 2 and not (first and h == 0):
                        if h == 0:
                            head_out(u - 1, HEADS - 1, i - 1, 1 - k, True)
                        else:
                            head_out(u - 1, h - 1, i, k, isinstance(i, int) and i < 2)

            for u in range(LEAD):
                for c in range(NS):
                    mask_part(u, u, 0, 0, c)
                maximum(u, u)
            for i in range(2):
                for h in range(HEADS):
                    unit(i, h, i, first=i == 0)
            with dve.Fori(1, NB // 2 - 1) as j:
                for k in range(2):
                    for h in range(HEADS):
                        unit(j * 2 + k, h, k)
            for i in (NB - 2, NB - 1):
                for h in range(HEADS):
                    unit(i, h, i % 2, last=i == NB - 1)
            head_out(UNITS - 1, HEADS - 1, NB - 1, 1, True)


def layer1_end(nc, t, m, dram):
    with ExitStack() as ctx:
        sb = lambda name, shape, dt=F32: ctx.enter_context(nc.sbuf_tensor("l1_" + name, shape, dt))
        sem = lambda name: ctx.enter_context(nc.semaphore("l1_" + name))
        out = sb("out", [P, NB, D])
        skip = sb("skip", [P, NB, D])
        diff = sb("diff", [P, NB, D])
        prod = sb("prod", [P, NB, D])
        logit = sb("logit", [P, 3, NB])
        beta = sb("beta", [P, 2, NB])
        stat = sb("stat", [P, 6, NB])
        turned = ctx.enter_context(nc.psum_tensor("l1_turned", [P, N], F32))
        loaded, logit_ready, beta_ready, var_ready, std_ready, h_ready, turned_ready, steps = (sem(n) for n in (
            "loaded", "logit_ready", "beta_ready", "var_ready", "std_ready", "h_ready", "turned_ready", "steps"))
        block = ctx.enter_context(nc.Block())

        @block.sync
        def _(sp):
            for to, of in ((out, dram.attended), (skip, dram.skip), (m.x, dram.x1)):
                sp.dma_start(to[:], of.rearrange("(b p) d -> p b d", p=P)).then_inc(loaded, 16)

        @block.vector
        def _(dve):
            step = Chain(dve, steps)
            dve.wait_ge(loaded, 48)
            step(dve.tensor_tensor(diff[:], out[:], skip[:], ALU.subtract))
            for k, v in enumerate((out, skip, diff)):
                w = m.w_beta[:, k * D:(k + 1) * D].unsqueeze(1).to_broadcast([P, NB, D])
                step(dve.tensor_tensor(prod[:], v[:], w, ALU.mult))
                step(dve.reduce_sum(logit[:, k, :], prod[:], AX_X))
            step(dve.tensor_tensor(logit[:, 0, :], logit[:, 0, :], logit[:, 1, :], ALU.add))
            dve.tensor_tensor(beta[:, 0, :], logit[:, 0, :], logit[:, 2, :], ALU.add).then_inc(logit_ready, 1)
            dve.wait_ge(beta_ready, 1)
            step(dve.tensor_tensor(diff[:], diff[:], over(beta[:, 1, :], NB), ALU.mult))
            step(dve.tensor_tensor(out[:], out[:], diff[:], ALU.subtract))
            step(dve.tensor_tensor(m.x[:], m.x[:], out[:], ALU.add))
            normalise(step, dve, m.x[:], m.h[:], diff[:], prod[:], stat, NB, var_ready, std_ready, 1).then_inc(h_ready, 1)

        @block.scalar
        def _(act):
            act.wait_ge(logit_ready, 1)
            act.activation(beta[:, 1, :], beta[:, 0, :], ACT.Sigmoid).then_inc(beta_ready, 1)
            root(act, stat, var_ready, std_ready, 1)
            for c in range(NCH):
                act.wait_ge(turned_ready, c + 1)
                act.activation(m.h_t[:, c * CW:(c + 1) * CW], turned[:, c * CW:(c + 1) * CW], ACT.Copy)

        @block.tensor
        def _(pe):
            pe.wait_ge(h_ready, 1)
            for c in range(NCH):
                for b in range(CB * c, CB * c + CB):
                    last = pe.transpose(turned[:, b * P:(b + 1) * P], m.h[:, b, :], m.ident[:])
                last.then_inc(turned_ready, 1)


def layer2(nc, t, m, dram):
    RING = 8
    with ExitStack() as ctx:
        sb = lambda name, shape, dt=F32: ctx.enter_context(nc.sbuf_tensor("l2_" + name, shape, dt))
        bank = lambda name, n=1: ctx.enter_context(nc.psum_tensor("l2_" + name, [P, n * CW], F32))
        sem = lambda name: ctx.enter_context(nc.semaphore("l2_" + name))
        a_in = sb("a_in", [P, RING, GR, CW])
        agg = sb("agg", [P, CW])
        msg = sb("msg", [P, CW])
        r, z, n_in, new, diff, = (sb(n, [P, CW]) for n in ("r", "z", "n_in", "new", "diff"))
        acc, msg_acc, r_acc, z_acc, in_acc, hn_acc = (bank(n) for n in ("acc", "msg_acc", "r_acc", "z_acc", "in_acc", "hn_acc"))
        loaded = [sem(f"loaded{s}") for s in range(RING)]
        grouped, agg_out, msg_acc_ready, msg_ready, r_acc_ready, z_acc_ready, n_acc_ready, r_ready, z_ready, n_sum_ready, n_ready, h_out, steps = (
            sem(n) for n in ("grouped", "agg_out", "msg_acc_ready", "msg_ready", "r_acc_ready", "z_acc_ready",
                             "n_acc_ready", "r_ready", "z_ready", "n_sum_ready", "n_ready", "h_out", "steps"))
        block = ctx.enter_context(nc.Block())
        at_rows = dram.adj_t.rearrange("(g r p) m -> g p r m", r=GR, p=P)
        W_MSG, W_I, W_H = 0, 1, 4
        w = lambda k: m.w_gru[:, k, :]

        @block.sync
        def _(sp):
            def body(c, first):
                for g in range(NG):
                    if not first:
                        wait_apart(sp, m.passed, grouped, NG * (c - 1) + g + 1)
                    sp.dma_start(a_in[:, g], at_rows[g, :, :, bass.ts(c, CW)]).then_inc(loaded[g], 16)
            body(0, True)
            with sp.Fori(1, NCH) as c:
                body(c, False)

        @block.tensor
        def _(pe):
            def gates(c):
                pe.wait_ge(agg_out, c + 1)
                pe.matmul(msg_acc[:], w(W_MSG), agg[:], start=True, stop=True).then_inc(msg_acc_ready, 1)
                h_c = m.h_t[:, bass.ts(c, CW)]
                pe.matmul(hn_acc[:], w(W_H + 2), h_c, start=True, stop=True)
                pe.matmul(r_acc[:], w(W_H), h_c, start=True, stop=False)
                pe.matmul(z_acc[:], w(W_H + 1), h_c, start=True, stop=False)
                pe.wait_ge(msg_ready, c + 1)
                pe.matmul(r_acc[:], w(W_I), msg[:], start=False, stop=True).then_inc(r_acc_ready, 1)
                pe.matmul(in_acc[:], w(W_I + 2), msg[:], start=True, stop=True).then_inc(n_acc_ready, 1)
                pe.matmul(z_acc[:], w(W_I + 1), msg[:], start=False, stop=True).then_inc(z_acc_ready, 1)

            def body(c, first):
                for g in range(NG):
                    pe.wait_ge(loaded[g], 16 * c + 16)
                    if g == 0 and not first:
                        pe.wait_ge(agg_out, c)
                    for k in range(GR):
                        last = pe.matmul(acc[:], m.h[:, g * GR + k, :], a_in[:, g, k, :], start=(g + k == 0),
                                         stop=(g == NG - 1 and k == GR - 1))
                    last.then_inc(grouped, 1)
                if not first:
                    pe.wait_ge(h_out, c)
                gates(c)
            body(0, True)
            with pe.Fori(1, NCH) as c:
                body(c, False)

        @block.scalar
        def _(act):
            with act.Fori(0, NCH) as c:
                act.wait_ge(grouped, NG * c + NG)
                act.activation(agg[:], acc[:], ACT.Copy).then_inc(agg_out, 1)
                act.wait_ge(msg_acc_ready, c + 1)
                act.activation(msg[:], msg_acc[:], ACT.Relu, bias=m.b_msg[:]).then_inc(msg_ready, 1)
                act.wait_ge(r_acc_ready, c + 1)
                act.activation(r[:], r_acc[:], ACT.Sigmoid, bias=m.b_rz[:, 0:1]).then_inc(r_ready, 1)
                act.wait_ge(z_acc_ready, c + 1)
                act.activation(z[:], z_acc[:], ACT.Sigmoid, bias=m.b_rz[:, 1:2]).then_inc(z_ready, 1)
                act.wait_ge(n_sum_ready, c + 1)
                act.activation(new[:], n_in[:], ACT.Tanh, bias=m.b_ih[:, 2:3]).then_inc(n_ready, 1)

        @block.vector
        def _(dve):
            with dve.Fori(0, NCH) as c:
                step = Chain(dve, steps, c * 3)
                dve.wait_ge(r_ready, c + 1)
                step(dve.scalar_tensor_tensor(n_in[:], hn_acc[:], m.b_hh[:, 2:3], r[:], ALU.add, ALU.mult))
                dve.wait_ge(n_acc_ready, c + 1)
                dve.tensor_tensor(n_in[:], n_in[:], in_acc[:], ALU.add).then_inc(n_sum_ready, 1)
                dve.wait_ge(n_ready, c + 1)
                h_c = m.h_t[:, bass.ts(c, CW)]
                step(dve.tensor_tensor(diff[:], h_c, new[:], ALU.subtract))
                dve.wait_ge(z_ready, c + 1)
                step(dve.tensor_tensor(diff[:], diff[:], z[:], ALU.mult))
                dve.tensor_tensor(h_c, new[:], diff[:], ALU.add).then_inc(h_out, 1)


def layer2_end(nc, t, m, dram):
    with ExitStack() as ctx:
        sb = lambda name, shape, dt=F32: ctx.enter_context(nc.sbuf_tensor("le_" + name, shape, dt))
        sem = lambda name: ctx.enter_context(nc.semaphore("le_" + name))
        centred = sb("centred", [P, NB, D])
        square = sb("square", [P, NB, D])
        stat = sb("stat", [P, 6, NB])
        turned = ctx.enter_context(nc.psum_tensor("le_turned", [P, N], F32))
        turned_ready, var_ready, std_ready, h_ready, back, h_t_ready, projected, steps, g_out = (sem(n) for n in (
            "turned_ready", "var_ready", "std_ready", "h_ready", "back", "h_t_ready", "projected", "steps", "g_out"))
        block = ctx.enter_context(nc.Block())

        @block.tensor
        def _(pe):
            for b in range(NB):
                last = pe.transpose(turned[:, b * P:(b + 1) * P], m.h_t[:, b * P:(b + 1) * P], m.ident[:])
            last.then_inc(turned_ready, 1)
            pe.wait_ge(h_ready, 1)
            for c in range(NCH):
                for b in range(CB * c, CB * c + CB):
                    last = pe.transpose(turned[:, b * P:(b + 1) * P], m.h[:, b, :], m.ident[:])
                last.then_inc(back, 1)
            pe.wait_ge(h_t_ready, NCH)
            for b in range(NB):
                if b >= 16:
                    pe.wait_ge(g_out, b // 2 - 7)
                q = b % 16
                last = pe.matmul(turned[:, q * 2 * D:(q + 1) * 2 * D], m.h_t[:, b * P:(b + 1) * P], m.w_io[:], start=True, stop=True)
                if b % 2:
                    last.then_inc(projected, 1)

        @block.vector
        def _(dve):
            step = Chain(dve, steps)
            dve.wait_ge(turned_ready, 1)
            step(dve.tensor_tensor(m.x[:], m.x[:], turned[:].rearrange("p (b d) -> p b d", b=NB), ALU.add))
            normalise(step, dve, m.x[:], m.h[:], centred[:], square[:], stat, NB, var_ready, std_ready, 1).then_inc(h_ready, 1)
            for j in range(NB // 2):
                dve.wait_ge(projected, j + 1)
                q = j % 8
                both = turned[:, q * 4 * D:(q + 1) * 4 * D].rearrange("p (b k d) -> p k b d", b=2, k=2)
                dve.tensor_copy(m.h[:, 2 * j:2 * j + 2, :], both[:, 0])
                dve.tensor_copy(m.g[:, 2 * j:2 * j + 2, :], both[:, 1]).then_inc(g_out, 1)

        @block.scalar
        def _(act):
            root(act, stat, var_ready, std_ready, 1)
            for c in range(NCH):
                act.wait_ge(back, c + 1)
                act.activation(m.h_t[:, c * CW:(c + 1) * CW], turned[:, c * CW:(c + 1) * CW], ACT.Copy).then_inc(h_t_ready, 1)


def layer3(nc, t, m, dram):
    RING = 8
    with ExitStack() as ctx:
        sb = lambda name, shape, dt=F32: ctx.enter_context(nc.sbuf_tensor("l3_" + name, shape, dt))
        bank = lambda name, n=1: ctx.enter_context(nc.psum_tensor("l3_" + name, [P, n * CW], F32))
        sem = lambda name: ctx.enter_context(nc.semaphore("l3_" + name))
        a_in = sb("a_in", [P, RING, GR, CW])
        total = sb("total", [P, 2, CW])
        part = sb("part", [P, 2, CW])
        agg = sb("agg", [P, 2, CW])
        deg = sb("deg", [P, 3, 2, CB])
        out_c = sb("out_c", [P, CB, D])
        term = sb("term", [P, CB, D])
        acc = [bank(f"acc{k}") for k in range(2)]
        node = [bank(f"node{k}") for k in range(2)]
        degree = bank("degree")
        loaded = [sem(f"loaded{s}") for s in range(RING)]
        grouped, summed, agg_out, total_ready, deg_ready, node_ready, out_ready, stored, steps = (sem(n) for n in (
            "grouped", "summed", "agg_out", "total_ready", "deg_ready", "node_ready", "out_ready", "stored", "steps"))
        block = ctx.enter_context(nc.Block())
        sides = (dram.adj_t.rearrange("(g r p) m -> g p r m", r=GR, p=P), t["adj"].rearrange("(g r p) m -> g p r m", r=GR, p=P))
        out_rows = dram.out.rearrange("(c b p) d -> c p b d", b=CB, p=P)
        STEPS = 7

        @block.sync
        def _(sp):
            def body(c, first):
                for k in range(2):
                    for g in range(NG):
                        if not (first and k == 0):
                            at = NG * (2 * c + k - 1) + g + 1
                            wait_apart(sp, m.passed, grouped, at)
                            wait_apart(sp, m.passed, summed, at)
                        sp.dma_start(a_in[:, g], sides[k][g, :, :, bass.ts(c, CW)]).then_inc(loaded[g], 16)
                    if k == 0 and not first:
                        wait_apart(sp, m.passed, out_ready, c)
                        sp.dma_start(out_rows[bass.ts(c - 1, 1)].squeeze(0), out_c[:]).then_inc(stored, 16)
            body(0, True)
            with sp.Fori(1, NCH) as c:
                body(c, False)
            wait_apart(sp, m.passed, out_ready, NCH)
            sp.dma_start(out_rows[NCH - 1], out_c[:]).then_inc(stored, 16)
            sp.wait_ge(stored, 16 * NCH)

        @block.tensor
        def _(pe):
            def end(c):
                pe.wait_ge(total_ready, 2 * c + 2)
                for k in range(2):
                    for b in range(CB):
                        last = pe.matmul(degree[:, k * CB + b:k * CB + b + 1], total[:, k, b * P:(b + 1) * P], m.ones[:, 0:1], start=True, stop=True)
                last.then_inc(deg_ready, 1)
                for k in range(2):
                    pe.wait_ge(agg_out, 2 * c + k + 1)
                    for b in range(CB):
                        last = pe.transpose(node[k][:, b * P:(b + 1) * P], agg[:, k, b * P:(b + 1) * P], m.ident[:])
                    last.then_inc(node_ready, 1)

            def body(c, first):
                for k in range(2):
                    state = (m.h, m.g)[k]
                    for g in range(NG):
                        pe.wait_ge(loaded[g], 32 * c + 16 * k + 16)
                        if g == 0 and not first:
                            pe.wait_ge(agg_out, 2 * c - 1 + k)
                        for r in range(GR):
                            last = pe.matmul(acc[k][:], state[:, g * GR + r, :], a_in[:, g, r, :], start=(g + r == 0),
                                             stop=(g == NG - 1 and r == GR - 1))
                        last.then_inc(grouped, 1)
                if not first:
                    pe.wait_ge(out_ready, c)
                end(c)
            body(0, True)
            with pe.Fori(1, NCH) as c:
                body(c, False)

        @block.scalar
        def _(act):
            def body(c, first):
                for k in range(2):
                    act.wait_ge(grouped, NG * (2 * c + k) + NG)
                    if not first:
                        act.wait_ge(node_ready, 2 * c - 1 + k)
                    act.activation(agg[:, k, :], acc[k][:], ACT.Copy).then_inc(agg_out, 1)
            body(0, True)
            with act.Fori(1, NCH) as c:
                body(c, False)

        @block.vector
        def _(dve):
            def body(c, first):
                step = Chain(dve, steps, STEPS * c)
                for k in range(2):
                    for g in range(NG):
                        dve.wait_ge(loaded[g], 32 * c + 16 * k + 16)
                        if g == 0 and k == 0 and not first:
                            dve.wait_ge(deg_ready, c)
                        to = total[:, k, :] if g == 0 else part[:, g % 2, :]
                        dve.reduce_sum(to, a_in[:, g].rearrange("p r n -> p n r"), AX_X).then_inc(summed, 1)
                        dve.wait_ge(summed, NG * (2 * c + k) + g + 1)
                        if g:
                            add = dve.tensor_tensor(total[:, k, :], total[:, k, :], part[:, g % 2, :], ALU.add)
                    add.then_inc(total_ready, 1)
                dve.wait_ge(deg_ready, c + 1)
                some, safe, inverse = (deg[:, k] for k in range(3))
                both = degree[:, 0:2 * CB].rearrange("p (k b) -> p k b", k=2)
                step(dve.tensor_scalar(some, both, 0.0, None, ALU.is_gt))
                step(dve.tensor_tensor(safe, both, some, ALU.mult))
                step(dve.tensor_scalar(some, some, -1.0, 1.0, ALU.mult, ALU.add))
                step(dve.tensor_tensor(safe, safe, some, ALU.add))
                step(dve.reciprocal(inverse, safe))
                if not first:
                    dve.wait_ge(stored, 16 * c)
                dve.wait_ge(node_ready, 2 * c + 2)
                as_nodes = lambda v: v[:].rearrange("p (b d) -> p b d", b=CB)
                step(dve.tensor_tensor(out_c[:], as_nodes(node[0]), over(inverse[:, 0, :], CB), ALU.mult))
                dve.tensor_tensor(term[:], as_nodes(node[1]), over(inverse[:, 1, :], CB), ALU.mult)
                step(dve.tensor_tensor(out_c[:], out_c[:], m.x[:, bass.ts(c, CB), :], ALU.add))
                dve.tensor_tensor(out_c[:], out_c[:], term[:], ALU.add).then_inc(out_ready, 1)
            body(0, True)
            with dve.Fori(1, NCH) as c:
                body(c, False)


def graph_layers(nc, t, out, phases=(setup, layer0, attention, layer1_end, layer2, layer2_end, layer3)):
    scratch = lambda name, shape: nc.dram_tensor(name, shape, F32, kind="Internal").ap()
    dram = Places()
    dram.adj_t, dram.out = scratch("adj_t", [N, N]), out
    dram.x1, dram.skip, dram.attended = (scratch(name, [N, D]) for name in ("x1", "skip", "attended"))
    dram.q_stack, dram.k_stack = (scratch(name, [HEADS, P, N]) for name in ("q_stack", "k_stack"))
    with ExitStack() as ctx:
        sb = lambda name, shape, dt=F32: ctx.enter_context(nc.sbuf_tensor(name, shape, dt))
        m = Places()
        m.ident, m.ident_sum, m.ones = sb("ident", [P, P]), sb("ident_sum", [P, HC]), sb("ones", [P, 1])
        m.w_q, m.w_k, m.w_vs = sb("w_q", [D, D]), sb("w_k", [D, D]), sb("w_vs", [D, 2 * D])
        m.w_io, m.w_gru, m.w_beta = sb("w_io", [D, 2 * D]), sb("w_gru", [D, 7, D]), sb("w_beta", [P, 3 * D])
        m.b_vs, m.b_q, m.b_k, m.b_msg = sb("b_vs", [P, 2 * D]), sb("b_q", [D, 1]), sb("b_k", [D, 1]), sb("b_msg", [D, 1])
        m.b_ih, m.b_hh, m.b_rz = sb("b_ih", [D, 3]), sb("b_hh", [D, 3]), sb("b_rz", [D, 2])
        m.passed = ctx.enter_context(nc.semaphore("passed"))
        with ExitStack() as attention_only:
            asb = lambda name, shape, dt=F32: attention_only.enter_context(nc.sbuf_tensor(name, shape, dt))
            m.k_stack = asb("k_stack_sb", [P, HEADS, N], F32R)
            m.v = asb("v", [P, NB, D])
            with nc.sbuf_tensor("h0", [P, NB, D], F32) as h0:
                m.h = h0
                for phase in phases[:2]:
                    phase(nc, t, m, dram)
            for phase in phases[2:3]:
                phase(nc, t, m, dram)
        m.h, m.x, m.g = (sb(name, [P, NB, D]) for name in ("h", "x", "g"))
        m.h_t = sb("later_h_t", [P, N])
        for phase in phases[3:]:
            phase(nc, t, m, dram)


_INS = ['x', 'adj', 'L1_gnn_Wq', 'L1_gnn_bq', 'L1_gnn_Wk', 'L1_gnn_bk', 'L1_gnn_Wv', 'L1_gnn_bv', 'L1_gnn_Ws',
        'L1_gnn_bs', 'L1_gnn_Wb', 'L2_gnn_W_msg', 'L2_gnn_b_msg', 'L2_gnn_W_ih', 'L2_gnn_W_hh', 'L2_gnn_b_ih',
        'L2_gnn_b_hh', 'L3_gnn_W_in', 'L3_gnn_W_out']


def kernel(**inputs):
    import numpy as np
    import concourse.bacc as bacc
    from concourse.bass_utils import run_bass_kernel_spmd

    nc = bacc.Bacc("TRN2", target_bir_lowering=False, num_devices=1)
    arrays, tensors = {}, {}
    for name in _INS:
        a = np.ascontiguousarray(inputs[name])
        arrays[name + "_in"] = a
        tensors[name] = nc.dram_tensor(name + "_in", a.shape, mybir.dt.from_np(a.dtype), kind="ExternalInput").ap()
    out = nc.dram_tensor("out", (N, D), F32, kind="ExternalOutput").ap()
    graph_layers(nc, tensors, out)
    return run_bass_kernel_spmd(nc, [arrays], core_ids=[0]).results[0]["out"]
```

```python
from contextlib import ExitStack

import concourse.bass as bass
from concourse import mybir

P = 128
N = 4096
D = 128
NB = N // P
CW = 512
NCH = N // CW
CB = CW // P
GR = 4
NG = NB // GR
HEADS = 4
HC = D // HEADS
SW = 1024
NS = N // SW
EPS = 1e-5
HIDE = -1.0e30
LOWEST = -3.0e38

F32 = mybir.dt.float32
F32R = mybir.dt.float32r
BF16 = mybir.dt.bfloat16
ALU = mybir.AluOpType
ACT = mybir.ActivationFunctionType
AX_X = mybir.AxisListType.X


class Places:
    pass


class Chain:

    def __init__(self, engine, sem, base=0):
        self.engine, self.sem, self.base, self.n = engine, sem, base, 0

    def __call__(self, instruction):
        self.n += 1
        instruction.then_inc(self.sem, 1)
        self.engine.wait_ge(self.sem, self.base + self.n)


def at(v, i):
    return v[i] if isinstance(i, int) else v[bass.ts(i, 1)].squeeze(0)


def wait_apart(engine, passed, sem, value):
    engine.wait_ge(sem, value)
    engine.sem_inc(passed, 1)


def over(stat, blocks):
    return stat.unsqueeze(2).to_broadcast([P, blocks, D])


def normalise(step, dve, x, h, centred, square, stat, blocks, var_ready, std_ready, turn):
    total, mean, var, std, inv, tmp = (stat[:, k, :] for k in range(6))
    step(dve.reduce_sum(total, x, AX_X))
    step(dve.tensor_scalar(mean, total, 1.0 / D, None, ALU.mult))
    step(dve.tensor_tensor(centred, x, over(mean, blocks), ALU.subtract))
    step(dve.tensor_tensor(square, centred, centred, ALU.mult))
    step(dve.reduce_sum(total, square, AX_X))
    dve.tensor_scalar(var, total, 1.0 / D, EPS, ALU.mult, ALU.add).then_inc(var_ready, 1)
    dve.wait_ge(std_ready, turn)
    step(dve.reciprocal(inv, std))
    step(dve.tensor_tensor(tmp, inv, inv, ALU.mult))
    step(dve.tensor_tensor(tmp, tmp, var, ALU.mult))
    step(dve.tensor_scalar(tmp, tmp, -0.5, 1.5, ALU.mult, ALU.add))
    step(dve.tensor_tensor(inv, inv, tmp, ALU.mult))
    return dve.scalar_tensor_tensor(h, centred, 0.0, over(inv, blocks), ALU.max, ALU.mult)


NORM_STEPS = 10


def root(act, stat, var_ready, std_ready, turn):
    act.wait_ge(var_ready, turn)
    act.activation(stat[:, 3, :], stat[:, 2, :], ACT.Sqrt).then_inc(std_ready, 1)


def layer0(nc, t, m, dram):
    RING = 4
    with ExitStack() as ctx:
        sb = lambda name, shape, dt=F32: ctx.enter_context(nc.sbuf_tensor("l0_" + name, shape, dt))
        bank = lambda name, n=1: ctx.enter_context(nc.psum_tensor("l0_" + name, [P, n * CW], F32))
        sem = lambda name: ctx.enter_context(nc.semaphore("l0_" + name))
        w_q, w_k, w_vs = sb("w_q", [D, D]), sb("w_k", [D, D]), sb("w_vs", [D, 2 * D])
        b_q, b_k, b_vs = sb("b_q", [D, 1]), sb("b_k", [D, 1]), sb("b_vs", [P, 2 * D])
        x = sb("x", [P, NB, D])
        h0 = sb("h0", [P, NB, D])
        raw = sb("raw", [P, 7, D])
        a_in = sb("a_in", [P, RING, GR, CW])
        colsum = sb("colsum", [P, CW])
        part = sb("part", [P, 2, CW])
        msg_t = sb("msg_t", [P, CW])
        x1 = sb("x1", [P, CB, D])
        h_c = sb("h_c", [P, CB, D])
        centred = sb("centred", [P, CB, D])
        square = sb("square", [P, CB, D])
        h_t = sb("h_t", [P, CW])
        full = sb("full", [P, 2, CW])
        high = sb("high", [P, 2, CW], F32R)
        low = sb("low", [P, 2, CW], F32R)
        skip = sb("skip", [P, CB, D])
        stat0 = sb("stat0", [P, 6, CB])
        stat = sb("stat", [P, 6, CB])
        deg = sb("deg", [P, 6, CB])
        acc = bank("acc")
        node = bank("node")
        proj = bank("proj", 2)
        turned = bank("turned", 2)
        x_loaded = [sem(f"x_loaded{g}") for g in range(NG)]
        loaded = [sem(f"loaded{s}") for s in range(RING)]
        (w_loaded, zeroed, ident_ready, weights_turned, var0_ready, std0_ready, h0_ready, grouped, summed, added,
         acc_ready, deg_ready, msg_out, msg_turned, x1_ready, x1_stored, var_ready, std_ready, h_ready, h_turned,
         ht_ready, qk_ready, qk_split, qk_stored, k_loaded, vs_ready, vs_out, skip_stored, steps0, steps) = (
            sem(n) for n in (
                "w_loaded", "zeroed", "ident_ready", "weights_turned", "var0_ready", "std0_ready", "h0_ready",
                "grouped", "summed", "added", "acc_ready", "deg_ready", "msg_out", "msg_turned", "x1_ready",
                "x1_stored", "var_ready", "std_ready", "h_ready", "h_turned", "ht_ready", "qk_ready", "qk_split",
                "qk_stored", "k_loaded", "vs_ready", "vs_out", "skip_stored", "steps0", "steps"))
        block = ctx.enter_context(nc.Block())
        a_rows = t["adj"].rearrange("(g r p) n -> g p r n", r=GR, p=P)
        x_groups = t["x"].rearrange("(g b p) d -> g p b d", b=CB, p=P)
        nodes = lambda v: v.rearrange("(c b p) d -> c p b d", b=CB, p=P)
        one_col = lambda v: v.rearrange("(p a) -> p a", a=1)
        weights = [
            (w_q[:], t["L1_gnn_Wq"]), (w_k[:], t["L1_gnn_Wk"]),
            (w_vs[:, 0:D], t["L1_gnn_Wv"]), (w_vs[:, D:2 * D], t["L1_gnn_Ws"]),
            (b_q[:], one_col(t["L1_gnn_bq"])), (b_k[:], one_col(t["L1_gnn_bk"])),
            (b_vs[:, 0:D], t["L1_gnn_bv"].partition_broadcast(P)), (b_vs[:, D:2 * D], t["L1_gnn_bs"].partition_broadcast(P)),
            (m.w_beta[:], t["L1_gnn_Wb"].rearrange("n o -> (n o)").partition_broadcast(P)),
            (raw[:, 0, :], t["L2_gnn_W_msg"]),
            (raw[:, 1:4, :], t["L2_gnn_W_ih"].rearrange("(g o) d -> o g d", g=3)),
            (raw[:, 4:7, :], t["L2_gnn_W_hh"].rearrange("(g o) d -> o g d", g=3)),
            (m.w_io[:, 0:D], t["L3_gnn_W_in"]), (m.w_io[:, D:2 * D], t["L3_gnn_W_out"]),
            (m.b_msg[:], one_col(t["L2_gnn_b_msg"])),
        ]
        for gate in range(3):
            rows = slice(gate * D, (gate + 1) * D)
            weights += [(m.b_ih[:, gate:gate + 1], one_col(t["L2_gnn_b_ih"][rows])),
                        (m.b_hh[:, gate:gate + 1], one_col(t["L2_gnn_b_hh"][rows]))]
        W_ALL = 16 * len(weights)
        K_STEPS = 9 + NORM_STEPS + 4

        def each(engine, body):
            body(0, None, True)
            body(1, 0, False)
            with engine.Fori(2, NCH) as c:
                body(c, c - 1, False)
            body(None, NCH - 1, False)

        @block.sync
        def _(sp):
            def load(c, g):
                sp.dma_start(a_in[:, g % RING], a_rows[g, :, :, bass.ts(c, CW)]).then_inc(loaded[g % RING], 16)

            for g in range(NG):
                sp.dma_start(x[:, g * CB:(g + 1) * CB, :], x_groups[g]).then_inc(x_loaded[g], 16)
                if g < RING:
                    load(0, g)

            def reload(c, g):
                sp.wait_ge(grouped, NG * c + g - RING + 1)
                wait_apart(sp, m.passed, summed, NG * c + g - RING + 1)
                load(c, g)

            for g in range(RING, NG):
                reload(0, g)
            with sp.Fori(1, NCH) as c:
                for g in range(NG):
                    reload(c, g)

        @block.tensor
        def _(pe):
            def stream(c, g, first):
                pe.wait_ge(loaded[g % RING], 16 * (NG // RING) * c + 16 * (g // RING) + 16)
                if first:
                    pe.wait_ge(h0_ready, g + 1)
                if g == 0 and not first:
                    pe.wait_ge(msg_out, c)
                for r in range(GR):
                    last = pe.matmul(acc[:], h0[:, GR * g + r, :], a_in[:, g % RING, r, :],
                                     start=(g == 0 and r == 0), stop=(g == NG - 1 and r == GR - 1))
                last.then_inc(grouped, 1)

            def turn_weights():
                pe.wait_ge(w_loaded, W_ALL)
                for k in range(7):
                    last = pe.transpose(turned[:, k * P:(k + 1) * P], raw[:, k, :], m.ident[:])
                last.then_inc(weights_turned, 1)

            def degrees_and_message(e, later):
                pe.wait_ge(added, NG * e + NG)
                if later:
                    pe.wait_ge(vs_out, e)
                for b in range(CB):
                    last = pe.matmul(proj[:, b:b + 1], colsum[:, b * P:(b + 1) * P], m.ones[:, 0:1], start=True, stop=True)
                last.then_inc(deg_ready, 1)
                pe.wait_ge(msg_out, e + 1)
                for b in range(CB):
                    last = pe.transpose(node[:, b * P:(b + 1) * P], msg_t[:, b * P:(b + 1) * P], m.ident[:])
                last.then_inc(msg_turned, 1)

            def turn_h(e):
                pe.wait_ge(h_ready, e + 1)
                for b in range(CB):
                    last = pe.transpose(node[:, b * P:(b + 1) * P], h_c[:, b, :], m.ident[:])
                last.then_inc(h_turned, 1)

            def project_qk(e):
                pe.wait_ge(ht_ready, e + 1)
                pe.matmul(proj[:, 0:CW], w_q[:], h_t[:], start=True, stop=True).then_inc(qk_ready, 1)
                pe.matmul(proj[:, CW:2 * CW], w_k[:], h_t[:], start=True, stop=True).then_inc(qk_ready, 1)

            def project_vs(e):
                pe.wait_ge(qk_split, 2 * e + 2)
                for b in range(CB):
                    last = pe.matmul(proj[:, b * 2 * D:(b + 1) * 2 * D], h_t[:, b * P:(b + 1) * P], w_vs[:],
                                     start=True, stop=True)
                last.then_inc(vs_ready, 1)

            def body(c, e, first):
                for g in range(NG):
                    if c is not None:
                        stream(c, g, first)
                    if e is not None:
                        if g == 1:
                            degrees_and_message(e, c is None or not isinstance(c, int))
                        elif g == 4:
                            turn_h(e)
                        elif g == 5:
                            project_qk(e)
                        elif g == 6:
                            project_vs(e)
                if first:
                    turn_weights()

            pe.wait_ge(ident_ready, 1)
            each(pe, body)

        @block.scalar
        def _(act):
            def copy_message(c):
                act.wait_ge(grouped, NG * c + NG)
                act.activation(msg_t[:], acc[:], ACT.Copy).then_inc(msg_out, 1)

            def behind(e):
                root(act, stat, var_ready, std_ready, e + 1)
                act.wait_ge(x1_ready, e + 1)
                act.dma_start(at(nodes(dram.x1), e), x1[:]).then_inc(x1_stored, 16)
                act.wait_ge(h_turned, e + 1)
                act.activation(h_t[:], node[:], ACT.Copy).then_inc(ht_ready, 1)
                for k, stack, order in ((0, dram.q_stack, (high, high, low, low)), (1, dram.k_stack, (high, low, high, low))):
                    act.wait_ge(qk_split, 2 * e + k + 1)
                    for s, half in enumerate(order):
                        to = stack[:, s * HC:(s + 1) * HC, bass.ts(e, CW)]
                        act.dma_start(to, half[:, k, :].bitcast(F32)).then_inc(qk_stored, 16)
                act.wait_ge(vs_out, e + 1)
                act.dma_start(at(nodes(dram.skip), e), skip[:]).then_inc(skip_stored, 16)

            def fetch_k(e):
                act.wait_ge(qk_stored, 128 * e + 128)
                act.dma_start(m.k_stack[:, :, bass.ts(e, CW)].bitcast(F32),
                              dram.k_stack[:, :, bass.ts(e, CW)].rearrange("h s n -> s h n")).then_inc(k_loaded, 16)

            for to, of in weights:
                act.dma_start(to, of).then_inc(w_loaded, 16)
            for g in range(NG):
                root(act, stat0, var0_ready, std0_ready, g + 1)
            copy_message(0)
            act.wait_ge(weights_turned, 1)
            act.activation(m.w_gru[:], turned[:, 0:7 * P].rearrange("p (k o) -> p k o", k=7), ACT.Copy)
            with act.Fori(1, NCH) as c:
                behind(c - 1)
                copy_message(c)
                fetch_k(c - 1)
            behind(NCH - 1)
            fetch_k(NCH - 1)
            for stored, n in ((x1_stored, 16), (skip_stored, 16), (k_loaded, 16)):
                act.wait_ge(stored, n * NCH)

        @block.vector
        def _(dve):
            def first_h(g, step):
                dve.wait_ge(x_loaded[g], 16)
                rows = slice(g * CB, (g + 1) * CB)
                step(normalise(step, dve, x[:, rows, :], h0[:, rows, :], centred[:], square[:], stat0, CB,
                               var0_ready, std0_ready, g + 1))
                dve.sem_inc(h0_ready, 1)

            def stream(c, g, first):
                dve.wait_ge(loaded[g % RING], 16 * (NG // RING) * c + 16 * (g // RING) + 16)
                if not (first and g < 2):
                    dve.wait_ge(added, NG * c + g - 1)
                dve.reduce_sum(part[:, g % 2, :], a_in[:, g % RING].rearrange("p r n -> p n r"), AX_X).then_inc(summed, 1)

            def add_message(e, step, later):
                dve.wait_ge(deg_ready, e + 1)
                empty, safe, inverse, some, safe3 = (deg[:, k, :] for k in range(5))
                total = proj[:, 0:CB]
                step(dve.tensor_scalar(empty, total, 0.0, None, ALU.is_equal))
                step(dve.tensor_tensor(safe, total, empty, ALU.add))
                step(dve.reciprocal(inverse, safe))
                step(dve.tensor_scalar(empty, empty, -1.0, 1.0, ALU.mult, ALU.add))
                step(dve.tensor_tensor(inverse, inverse, empty, ALU.mult))
                step(dve.tensor_scalar(some, total, 0.0, None, ALU.is_gt))
                dve.tensor_tensor(safe3, total, some, ALU.mult)
                step(dve.tensor_scalar(some, some, -1.0, 1.0, ALU.mult, ALU.add))
                step(dve.tensor_tensor(safe3, safe3, some, ALU.add))
                dve.reciprocal(m.col_inv[:, bass.ts(e, CB)], safe3)
                dve.wait_ge(msg_turned, e + 1)
                if later:
                    dve.wait_ge(x1_stored, 16 * e)
                step(dve.tensor_tensor(h_c[:], node[:].rearrange("p (b d) -> p b d", b=CB), over(inverse, CB), ALU.mult))
                dve.tensor_tensor(x1[:], x[:, bass.ts(e, CB), :], h_c[:], ALU.add).then_inc(x1_ready, 1)
                dve.wait_ge(x1_ready, e + 1)
                normalise(step, dve, x1[:], h_c[:], centred[:], square[:], stat, CB, var_ready, std_ready, e + 1)\
                    .then_inc(h_ready, 1)

            def split_qk(e, step, later):
                if later:
                    dve.wait_ge(qk_stored, 128 * e)
                for k in range(2):
                    dve.wait_ge(qk_ready, 2 * e + k + 1)
                    if k == 0:
                        step(dve.tensor_scalar(full[:, 0, :], proj[:, 0:CW], b_q[:], float(HC) ** -0.5, ALU.add, ALU.mult))
                    else:
                        step(dve.tensor_scalar(full[:, 1, :], proj[:, CW:2 * CW], b_k[:], None, ALU.add))
                    step(dve.tensor_copy(high[:, k, :], full[:, k, :]))
                    dve.tensor_tensor(low[:, k, :], full[:, k, :], high[:, k, :].bitcast(F32), ALU.subtract).then_inc(qk_split, 1)

            def add_vs(e, later):
                dve.wait_ge(vs_ready, e + 1)
                if later:
                    dve.wait_ge(skip_stored, 16 * e)
                vs = proj[:].rearrange("p (b k d) -> p b k d", b=CB, k=2)
                bias = lambda k: b_vs[:, k * D:(k + 1) * D].unsqueeze(1).to_broadcast([P, CB, D])
                dve.tensor_tensor(m.v[:, bass.ts(e, CB), :], vs[:, :, 0, :], bias(0), ALU.add)
                dve.tensor_tensor(skip[:], vs[:, :, 1, :], bias(1), ALU.add).then_inc(vs_out, 1)

            def body(c, e, first):
                later = e is not None and not (isinstance(e, int) and e == 0)
                step = Chain(dve, steps0) if first else Chain(dve, steps, K_STEPS * e)
                for g in range(NG):
                    if first:
                        first_h(g, step)
                    if c is not None:
                        stream(c, g, first)
                    if e is not None:
                        if g == 1:
                            add_message(e, step, later)
                        elif g == 5:
                            split_qk(e, step, later)
                        elif g == 6:
                            add_vs(e, later)
                assert first or step.n == K_STEPS, step.n
                if first:
                    dve.wait_ge(w_loaded, W_ALL)
                    dve.tensor_tensor(m.b_rz[:], m.b_ih[:, 0:2], m.b_hh[:, 0:2], ALU.add)

            each(dve, body)

        @block.gpsimd
        def _(pool):
            pool.memset(m.ident[:], 0.0).then_inc(zeroed, 1)
            pool.memset(m.ones[:], 1.0)
            pool.wait_ge(zeroed, 1)
            pool.affine_select(out=m.ident[:], in_=m.ident[:], compare_op=ALU.not_equal, fill=1.0, base=0,
                               pattern=[[-1, P]], channel_multiplier=1).then_inc(ident_ready, 1)
            pool.wait_ge(ident_ready, 1)
            pool.tensor_tensor(m.ident_sum[:], m.ident[:, 0:HC], m.ident[:, HC:2 * HC], ALU.add).then_inc(zeroed, 1)
            for k in range(2, 4):
                pool.wait_ge(zeroed, k)
                pool.tensor_tensor(m.ident_sum[:], m.ident_sum[:], m.ident[:, k * HC:(k + 1) * HC], ALU.add).then_inc(zeroed, 1)

            def body(c, first):
                for g in range(NG):
                    if g == 0 and not first:
                        pool.wait_ge(deg_ready, c)
                    wait_apart(pool, m.passed, summed, NG * c + g + 1)
                    if g == 0:
                        pool.tensor_copy(colsum[:], part[:, 0, :]).then_inc(added, 1)
                    else:
                        pool.wait_ge(added, NG * c + g)
                        pool.tensor_tensor(colsum[:], colsum[:], part[:, g % 2, :], ALU.add).then_inc(added, 1)

            body(0, True)
            with pool.Fori(1, NCH) as c:
                body(c, False)


def attention(nc, t, m, dram):
    UNITS = HEADS * NB
    LEAD = 2
    GC = 4
    G = NB // GC
    PARTS = N // CW
    BY_DVE = (1, 7)
    with ExitStack() as ctx:
        sb = lambda name, shape, dt=F32: ctx.enter_context(nc.sbuf_tensor("at_" + name, shape, dt))
        bank = lambda name, n=1: ctx.enter_context(nc.psum_tensor("at_" + name, [P, n * CW], F32))
        sem = lambda name: ctx.enter_context(nc.semaphore("at_" + name))
        a_in = sb("a_in", [P, N])
        mask = sb("mask", [P, 2, N], BF16)
        q_in = sb("q_in", [P, HEADS, P], F32R)
        probs = sb("probs", [P, HEADS, N])
        stage = sb("stage", [P, 2, 2 * GC, P])
        top = sb("top", [P, HEADS, PARTS])
        neg = sb("neg", [P, 2, HEADS])
        sums = sb("sums", [P, HEADS, NS])
        total = sb("total", [P, 3])
        tiles = sb("tiles", [P, 2, P])
        both = sb("both", [P, 2, 3, D])
        x = sb("x", [P, 2, D])
        product = sb("product", [P, 3 * D], BF16)
        gate = sb("gate", [P, 5])
        scores = [bank(f"scores{k}") for k in range(2)]
        turned = [bank(f"turned{k}") for k in range(4)]
        value = [bank(f"value{k}") for k in range(2)]
        a_loaded = [sem(f"a_loaded{c}") for c in range(NS)]
        q_loaded = [sem(f"q_loaded{h}") for h in range(HEADS)]
        x_loaded = [sem(f"x_loaded{k}") for k in range(2)]
        x_stored = [sem(f"x_stored{k}") for k in range(2)]
        stage_stored = [sem(f"stage_stored{k}") for k in range(2)]
        (a_turned, a_dve, a_act, logit_ready, gate_ready, x2_ready, gate_steps, first_mask, mask_ready, scores_ready,
         masked, max_ready, bias_ready, exp_ready, transposed, act_copied, dve_copied, tiled, tiles_out, summed,
         out_ready, steps) = (sem(n) for n in (
             "a_turned", "a_dve", "a_act", "logit_ready", "gate_ready", "x2_ready", "gate_steps", "first_mask",
             "mask_ready", "scores_ready", "masked", "max_ready", "bias_ready", "exp_ready", "transposed",
             "act_copied", "dve_copied", "tiled", "tiles_out", "summed", "out_ready", "steps"))
        block = ctx.enter_context(nc.Block())
        a_rows = t["adj"].rearrange("(b p) n -> b p n", p=P)
        blocks = lambda v: v.rearrange("(b p) d -> b p d", p=P)
        at_rows = dram.adj_t.rearrange("(h j p) n -> h p j n", j=2 * GC, p=P)

        def bank_of(h, s):
            return turned[(s + 2 * (h % 2)) % 4]

        def bank_of_group(h, g):
            return bank_of(h, g if g < 4 else g + 2)

        def wait_copied(engine, u, g):
            if g < 0:
                u, g = u - 1, g + G
            mine = sum(k <= g for k in BY_DVE)
            if g in BY_DVE:
                engine.wait_ge(dve_copied, len(BY_DVE) * u + mine)
            else:
                engine.wait_ge(act_copied, (G - len(BY_DVE)) * u + g + 1 - mine)

        @block.sync
        def _(sp):
            def load_a(i, h, first=False):
                if not first:
                    wait_apart(sp, m.passed, a_turned, 2 * (HEADS * (i - 1) + h) + 2)
                    if isinstance(i, int) and i == 1:
                        wait_apart(sp, m.passed, first_mask, h + 1)
                    else:
                        wait_apart(sp, m.passed, mask_ready, NS * (i - 2) + h + 1)
                sp.dma_start(a_in[:, h * SW:(h + 1) * SW], at(a_rows, i)[:, h * SW:(h + 1) * SW]).then_inc(a_loaded[h], 16)

            def load_q(i, h, first=False):
                if not first:
                    wait_apart(sp, m.passed, scores_ready, PARTS * (HEADS * (i - 1) + h) + PARTS)
                sp.dma_start(q_in[:, h, :].bitcast(F32), dram.q_stack[h, :, bass.ts(i, P)]).then_inc(q_loaded[h], 16)

            def store_stage(i, h):
                wait_apart(sp, m.passed, a_dve, HEADS * i + h + 1)
                wait_apart(sp, m.passed, a_act, HEADS * i + h + 1)
                sp.dma_start(at_rows[h, :, :, bass.ts(i, P)], stage[:, h % 2]).then_inc(stage_stored[h % 2], 16)

            def load_x(i, k, first=False):
                if not first:
                    wait_apart(sp, m.passed, x_stored[k], 8 * (i - k))
                sp.dma_start(both[:, k, 1, :], at(blocks(dram.skip), i)).then_inc(x_loaded[k], 16)
                sp.dma_start(x[:, k, :], at(blocks(dram.x1), i)).then_inc(x_loaded[k], 16)

            def store_x(i, k):
                wait_apart(sp, m.passed, x2_ready, i + 1)
                sp.dma_start(at(blocks(dram.x2), i), x[:, k, :]).then_inc(x_stored[k], 16)

            def period(i, k):
                for h in range(HEADS):
                    if not (isinstance(i, int) and i == NB - 1):
                        load_q(i + 1, h)
                        store_stage(i + 1, h)
                    if not (isinstance(i, int) and i >= NB - 2):
                        load_a(i + 2, h)
                    if h == 3 and not (isinstance(i, int) and i == 0):
                        store_x(i - 1, 1 - k)
                    if h == 3 and not (isinstance(i, int) and i == NB - 1):
                        load_x(i + 1, 1 - k, isinstance(i, int) and i == 0)

            for h in range(HEADS):
                load_q(0, h, True)
                load_a(0, h, True)
            load_x(0, 0, True)
            for h in range(HEADS):
                store_stage(0, h)
                load_a(1, h)
            for i in range(2):
                period(i, i)
            with sp.Fori(1, NB // 2 - 1) as j:
                for k in range(2):
                    period(j * 2 + k, k)
            for i in (NB - 2, NB - 1):
                period(i, i % 2)
            store_x(NB - 1, 1)
            for k in range(2):
                sp.wait_ge(x_stored[k], 16 * (NB // 2))
                sp.wait_ge(stage_stored[k], 16 * (NB * HEADS // 2))

        @block.gpsimd
        def _(pool):
            def make(i, k, first=False):
                for c in range(NS):
                    if c == 0 and not first:
                        pool.wait_ge(masked, PARTS * HEADS * (i - 1))
                    wait_apart(pool, m.passed, a_loaded[c], 16 * i + 16)
                    pool.tensor_scalar(mask[:, k, c * SW:(c + 1) * SW], a_in[:, c * SW:(c + 1) * SW], 0.0, HIDE,
                                       ALU.is_equal, ALU.mult).then_inc(mask_ready, 1)

            make(1, 1, True)
            with pool.Fori(1, NB // 2) as j:
                for k in range(2):
                    make(j * 2 + k, k)

        @block.tensor
        def _(pe):
            def score(u, h, i, p, first=False):
                if p == 0:
                    pe.wait_ge(q_loaded[h], 16 * i + 16)
                if not (first and p < 2):
                    pe.wait_ge(masked, PARTS * u + p - 1)
                pe.matmul(scores[p % 2][:], q_in[:, h, :], m.k_stack[:, h, p * CW:(p + 1) * CW],
                          start=True, stop=True).then_inc(scores_ready, 1)

            def values(u, h, g):
                if g < 0:
                    u, h, g = u - 1, (h - 1) % HEADS, g + G
                if g == 0 and not (isinstance(u, int) and u < 2):
                    pe.wait_ge(out_ready, u - 1)
                for r in range(GC):
                    part = slice((g * GC + r) * P, (g * GC + r + 1) * P)
                    last = pe.matmul(value[h % 2][r * HC:(r + 1) * HC, 0:P], m.v[:, g * GC + r, h * HC:(h + 1) * HC],
                                     probs[:, h, part], start=(g == 0), stop=(g == G - 1))
                if g == G - 1:
                    last.then_inc(tiled, 1)

            def add_tiles(u, k):
                pe.wait_ge(tiles_out, u + 1)
                pe.matmul(value[k][:, P:P + HC], tiles[:, k, :], m.ident_sum[:], start=True, stop=True).then_inc(summed, 1)

            def turn_a(i, h, first=False):
                pe.wait_ge(a_loaded[h], 16 * i + 16)
                for half in range(2):
                    if first and h >= 2:
                        pe.wait_ge((a_dve, a_act)[half], h - 1)
                    to = bank_of(h, 4 + half)
                    for r in range(GC):
                        col = h * SW + (half * GC + r) * P
                        last = pe.transpose(to[:, r * P:(r + 1) * P], a_in[:, col:col + P], m.ident[:])
                    last.then_inc(a_turned, 1)

            def turn(u, h, g):
                to = bank_of_group(h, g)
                for r in range(GC):
                    last = pe.transpose(to[:, r * P:(r + 1) * P],
                                        probs[:, h, (g * GC + r) * P:(g * GC + r + 1) * P], m.ident[:])
                last.then_inc(transposed, 1)

            def unit(i, h, first=False, last=False):
                u = i * HEADS + h
                begun = not (first and h == 0)
                scored = not (last and h >= HEADS - LEAD)
                ahead = lambda p: score(u + LEAD, (h + LEAD) % HEADS, i + (h + LEAD) // HEADS, p)
                for g in range(0, G, 2):
                    if scored:
                        ahead(g)
                    if g == 4:
                        wait_copied(pe, u, 0)
                        wait_copied(pe, u, 1)
                        if not last:
                            turn_a(i + 1, h)
                    pe.wait_ge(exp_ready, NS * u + g // 2 + 1)
                    for k in range(2):
                        if g < 4 and begun:
                            wait_copied(pe, u, g + k - 4)
                        elif g < 4:
                            pe.wait_ge((a_dve, a_act)[k], 3 + g // 2)
                        elif g == 4:
                            wait_copied(pe, u, 2 + k)
                        elif not last:
                            pe.wait_ge((a_dve, a_act)[k], u + HEADS + 1)
                        turn(u, h, g + k)
                    if g == 6 and begun:
                        add_tiles(u - 1, (h - 1) % 2)
                    if scored:
                        ahead(g + 1)
                    if begun or g >= 4:
                        values(u, h, g - 4)
                        values(u, h, g - 3)

            for c in range(NS):
                turn_a(0, c, first=True)
                for p in (2 * c, 2 * c + 1):
                    score(0, 0, 0, p, first=True)
            for p in range(PARTS):
                score(1, 1, 0, p)
            for h in range(HEADS):
                unit(0, h, first=True)
            with pe.Fori(1, NB - 1) as i:
                for h in range(HEADS):
                    unit(i, h)
            for h in range(HEADS):
                unit(NB - 1, h, last=True)
            for g in range(G - 4, G):
                wait_copied(pe, UNITS - 1, g)
                values(UNITS - 1, HEADS - 1, g)
            add_tiles(UNITS - 1, 1)

        @block.scalar
        def _(act):
            def exponentials(u, h, c):
                if c == 0:
                    act.wait_ge(bias_ready, u + 1)
                act.activation(probs[:, h, c * SW:(c + 1) * SW], probs[:, h, c * SW:(c + 1) * SW], ACT.Exp,
                               bias=neg[:, 1, h:h + 1], accum_out=sums[:, h, c:c + 1]).then_inc(exp_ready, 1)

            def copy_a(i, h, first=False):
                act.wait_ge(a_turned, 2 * (HEADS * i + h) + 2)
                if not (first and h < 2):
                    act.wait_ge(stage_stored[h % 2], 16 * (2 * i + h // 2))
                act.activation(stage[:, h % 2, GC:, :], bank_of(h, 5)[:].rearrange("p (j n) -> p j n", n=P), ACT.Copy)\
                    .then_inc(a_act, 1)

            def exp_of_gate(i):
                act.wait_ge(logit_ready, i + 1)
                act.activation(gate[:, 2:3], gate[:, 1:2], ACT.Exp, scale=-1.0).then_inc(gate_ready, 1)

            def tiles_of(u, k):
                act.wait_ge(tiled, u + 1)
                act.activation(tiles[:, k, :], value[k][:, 0:P], ACT.Copy).then_inc(tiles_out, 1)

            def unit(i, h, first=False, last=False):
                u = i * HEADS + h
                for c in range(NS):
                    for g in (2 * c, 2 * c + 1):
                        if g not in BY_DVE:
                            act.wait_ge(transposed, G * u + g + 1)
                            act.activation(probs[:, h, g * CW:(g + 1) * CW], bank_of_group(h, g)[:], ACT.Copy)\
                                .then_inc(act_copied, 1)
                    if not (last and h == HEADS - 1):
                        exponentials(u + 1, (h + 1) % HEADS, c)
                    if c == 1 and not (first and h == 0):
                        tiles_of(u - 1, (h - 1) % 2)
                    if c == 1 and not last:
                        copy_a(i + 1, h)
                    if c == 3 and h == 2 and not first:
                        exp_of_gate(i - 1)

            for h in range(HEADS):
                copy_a(0, h, first=True)
            for c in range(NS):
                exponentials(0, 0, c)
            for h in range(HEADS):
                unit(0, h, first=True)
            with act.Fori(1, NB - 1) as i:
                for h in range(HEADS):
                    unit(i, h)
            for h in range(HEADS):
                unit(NB - 1, h, last=True)
            tiles_of(UNITS - 1, 1)
            exp_of_gate(NB - 1)

        @block.vector
        def _(dve):
            def mask_part(u, h, i, k, p):
                if h == 0 and p % 2 == 0 and not (isinstance(i, int) and i == 0):
                    dve.wait_ge(mask_ready, NS * (i - 1) + p // 2 + 1)
                wait_apart(dve, m.passed, scores_ready, PARTS * u + p + 1)
                part = slice(p * CW, (p + 1) * CW)
                dve.tensor_tensor_reduce(
                    out=probs[:, h, part], in0=scores[p % 2][:], in1=mask[:, k, part],
                    scale=1.0, scalar=LOWEST, op0=ALU.add, op1=ALU.max, accum_out=top[:, h, p:p + 1]).then_inc(masked, 1)

            def maximum(u, h):
                dve.wait_ge(masked, PARTS * u + PARTS)
                dve.tensor_reduce(neg[:, 0, h:h + 1], top[:, h, :], AX_X, ALU.max, negate=True).then_inc(max_ready, 1)

            def bias_of(u, h):
                dve.wait_ge(max_ready, u + 1)
                dve.scalar_tensor_tensor(neg[:, 1, h:h + 1], neg[:, 0, h:h + 1], -HIDE / 2, neg[:, 0, h:h + 1],
                                         ALU.is_lt, ALU.mult).then_inc(bias_ready, 1)

            def copy_out(u, h, g):
                dve.wait_ge(transposed, G * u + g + 1)
                dve.tensor_copy(probs[:, h, g * CW:(g + 1) * CW], bank_of_group(h, g)[:]).then_inc(dve_copied, 1)

            def copy_a(i, h, first=False):
                dve.wait_ge(a_turned, 2 * (HEADS * i + h) + 1)
                if not (first and h < 2):
                    dve.wait_ge(stage_stored[h % 2], 16 * (2 * i + h // 2))
                dve.tensor_copy(stage[:, h % 2, 0:GC, :], bank_of(h, 4)[:].rearrange("p (j n) -> p j n", n=P)).then_inc(a_dve, 1)

            def gate_steps_of(i, k):
                done = 5 * i

                def difference():
                    dve.wait_ge(out_ready, HEADS * i + HEADS)
                    dve.wait_ge(x_loaded[k], 16 * (i - k) + 32)
                    dve.tensor_tensor(both[:, k, 2, :], both[:, k, 0, :], both[:, k, 1, :], ALU.subtract).then_inc(gate_steps, 1)

                def logit():
                    dve.wait_ge(gate_steps, done + 1)
                    dve.tensor_tensor_reduce(out=product[:], in0=both[:, k].rearrange("p k d -> p (k d)"), in1=m.w_beta[:],
                                             scale=1.0, scalar=0.0, op0=ALU.mult, op1=ALU.add,
                                             accum_out=gate[:, 0:1]).then_inc(gate_steps, 1)

                def bound():
                    dve.wait_ge(gate_steps, done + 2)
                    dve.tensor_scalar(gate[:, 1:2], gate[:, 0:1], -80.0, None, ALU.max).then_inc(logit_ready, 1)

                def one_more():
                    dve.wait_ge(gate_ready, i + 1)
                    dve.tensor_scalar(gate[:, 3:4], gate[:, 2:3], 1.0, None, ALU.add).then_inc(gate_steps, 1)

                def beta():
                    dve.wait_ge(gate_steps, done + 3)
                    dve.reciprocal(gate[:, 4:5], gate[:, 3:4]).then_inc(gate_steps, 1)

                def scaled():
                    dve.wait_ge(gate_steps, done + 4)
                    dve.tensor_tensor(x[:, k, :], x[:, k, :], both[:, k, 0, :], ALU.add)
                    dve.tensor_scalar(both[:, k, 2, :], both[:, k, 2, :], gate[:, 4:5], None, ALU.mult).then_inc(gate_steps, 1)

                def finish():
                    dve.wait_ge(gate_steps, done + 5)
                    dve.tensor_tensor(x[:, k, :], x[:, k, :], both[:, k, 2, :], ALU.subtract).then_inc(x2_ready, 1)

                return difference, logit, bound, one_more, beta, scaled, finish

            def head_steps_of(u, h, k):
                done = 3 * u

                def sum_up():
                    dve.wait_ge(exp_ready, NS * u + NS)
                    dve.reduce_sum(total[:, 0:1], sums[:, h, :], AX_X).then_inc(steps, 1)

                def safe():
                    dve.wait_ge(steps, done + 1)
                    dve.scalar_tensor_tensor(total[:, 1:2], total[:, 0:1], 0.0, total[:, 0:1], ALU.is_equal, ALU.add)\
                        .then_inc(steps, 1)

                def invert():
                    dve.wait_ge(steps, done + 2)
                    dve.reciprocal(total[:, 2:3], total[:, 1:2]).then_inc(steps, 1)

                def scale():
                    dve.wait_ge(steps, done + 3)
                    dve.wait_ge(summed, u + 1)
                    result = both[:, k, 0, :].rearrange("p (c h) -> p c h", h=HEADS)
                    dve.tensor_scalar(result[:, :, h], value[h % 2][:, P:P + HC], total[:, 2:3], None, ALU.mult)\
                        .then_inc(out_ready, 1)

                return sum_up, safe, invert, scale

            def unit(i, h, k, first=False, last=False):
                u = i * HEADS + h
                after = h + LEAD
                if not (first and h == 0):
                    sum_up, safe, invert, scale = head_steps_of(u - 1, (h - 1) % HEADS, k if h else 1 - k)
                if not first:
                    difference, logit, bound, one_more, beta, scaled, finish = gate_steps_of(i - 1, 1 - k)
                for g in range(G):
                    if not (last and after >= HEADS):
                        mask_part(u + LEAD, after % HEADS, i + after // HEADS, (k + after // HEADS) % 2, g)
                    if g < 2 and not (last and h == HEADS - 1):
                        (maximum, bias_of)[g](u + 1, (h + 1) % HEADS)
                    if g in BY_DVE:
                        copy_out(u, h, g)
                    if g == 4 and not last:
                        copy_a(i + 1, h)
                    if g in (2, 3, 5, 7) and not (first and h == 0):
                        {2: sum_up, 3: safe, 5: invert, 7: scale}[g]()
                    if h == 1 and g in (4, 5, 6) and not first:
                        (difference, logit, bound)[g - 4]()
                    if h == 3 and g in (3, 4, 5, 6) and not first:
                        (one_more, beta, scaled, finish)[g - 3]()

            for c in range(NS):
                part = slice(c * SW, (c + 1) * SW)
                dve.wait_ge(a_loaded[c], 16)
                dve.tensor_scalar(mask[:, 0, part], a_in[:, part], 0.0, HIDE, ALU.is_equal, ALU.mult).then_inc(first_mask, 1)
                copy_a(0, c, first=True)
                dve.wait_ge(first_mask, c + 1)
                for p in (2 * c, 2 * c + 1):
                    mask_part(0, 0, 0, 0, p)
            maximum(0, 0)
            bias_of(0, 0)
            for p in range(PARTS):
                mask_part(1, 1, 0, 0, p)
            for i in range(2):
                for h in range(HEADS):
                    unit(i, h, i, first=i == 0)
            with dve.Fori(1, NB // 2 - 1) as j:
                for k in range(2):
                    for h in range(HEADS):
                        unit(j * 2 + k, h, k)
            for i in (NB - 2, NB - 1):
                for h in range(HEADS):
                    unit(i, h, i % 2, last=i == NB - 1)
            for step in head_steps_of(UNITS - 1, HEADS - 1, 1) + gate_steps_of(NB - 1, 1):
                step()



def layer1_end(nc, t, m, dram):
    with ExitStack() as ctx:
        sb = lambda name, shape, dt=F32: ctx.enter_context(nc.sbuf_tensor("l1_" + name, shape, dt))
        sem = lambda name: ctx.enter_context(nc.semaphore("l1_" + name))
        diff = sb("diff", [P, NB, D])
        prod = sb("prod", [P, NB, D])
        stat = sb("stat", [P, 6, NB])
        turned = ctx.enter_context(nc.psum_tensor("l1_turned", [P, N], F32))
        loaded, var_ready, std_ready, h_ready, turned_ready, steps = (sem(n) for n in (
            "loaded", "var_ready", "std_ready", "h_ready", "turned_ready", "steps"))
        block = ctx.enter_context(nc.Block())

        @block.sync
        def _(sp):
            sp.dma_start(m.x[:], dram.x2.rearrange("(b p) d -> p b d", p=P)).then_inc(loaded, 16)

        @block.vector
        def _(dve):
            step = Chain(dve, steps)
            dve.wait_ge(loaded, 16)
            normalise(step, dve, m.x[:], m.h[:], diff[:], prod[:], stat, NB, var_ready, std_ready, 1).then_inc(h_ready, 1)

        @block.scalar
        def _(act):
            root(act, stat, var_ready, std_ready, 1)
            for c in range(NCH):
                act.wait_ge(turned_ready, c + 1)
                act.activation(m.h_t[:, c * CW:(c + 1) * CW], turned[:, c * CW:(c + 1) * CW], ACT.Copy)

        @block.tensor
        def _(pe):
            pe.wait_ge(h_ready, 1)
            for c in range(NCH):
                for b in range(CB * c, CB * c + CB):
                    last = pe.transpose(turned[:, b * P:(b + 1) * P], m.h[:, b, :], m.ident[:])
                last.then_inc(turned_ready, 1)


def layer2(nc, t, m, dram):
    RING = 8
    with ExitStack() as ctx:
        sb = lambda name, shape, dt=F32: ctx.enter_context(nc.sbuf_tensor("l2_" + name, shape, dt))
        bank = lambda name, n=1: ctx.enter_context(nc.psum_tensor("l2_" + name, [P, n * CW], F32))
        sem = lambda name: ctx.enter_context(nc.semaphore("l2_" + name))
        a_in = sb("a_in", [P, RING, GR, CW])
        agg = sb("agg", [P, CW])
        msg = sb("msg", [P, CW])
        r, z, n_in, new, diff, = (sb(n, [P, CW]) for n in ("r", "z", "n_in", "new", "diff"))
        acc, msg_acc, r_acc, z_acc, in_acc, hn_acc = (bank(n) for n in ("acc", "msg_acc", "r_acc", "z_acc", "in_acc", "hn_acc"))
        loaded = [sem(f"loaded{s}") for s in range(RING)]
        grouped, agg_out, msg_acc_ready, msg_ready, r_acc_ready, z_acc_ready, n_acc_ready, r_ready, z_ready, n_sum_ready, n_ready, h_out, steps = (
            sem(n) for n in ("grouped", "agg_out", "msg_acc_ready", "msg_ready", "r_acc_ready", "z_acc_ready",
                             "n_acc_ready", "r_ready", "z_ready", "n_sum_ready", "n_ready", "h_out", "steps"))
        block = ctx.enter_context(nc.Block())
        at_rows = dram.adj_t.rearrange("(g r p) m -> g p r m", r=GR, p=P)
        W_MSG, W_I, W_H = 0, 1, 4
        w = lambda k: m.w_gru[:, k, :]

        @block.sync
        def _(sp):
            def body(c, first):
                for g in range(NG):
                    if not first:
                        wait_apart(sp, m.passed, grouped, NG * (c - 1) + g + 1)
                    sp.dma_start(a_in[:, g], at_rows[g, :, :, bass.ts(c, CW)]).then_inc(loaded[g], 16)
            body(0, True)
            with sp.Fori(1, NCH) as c:
                body(c, False)

        @block.tensor
        def _(pe):
            def gates(c):
                pe.wait_ge(agg_out, c + 1)
                pe.matmul(msg_acc[:], w(W_MSG), agg[:], start=True, stop=True).then_inc(msg_acc_ready, 1)
                h_c = m.h_t[:, bass.ts(c, CW)]
                pe.matmul(hn_acc[:], w(W_H + 2), h_c, start=True, stop=True)
                pe.matmul(r_acc[:], w(W_H), h_c, start=True, stop=False)
                pe.matmul(z_acc[:], w(W_H + 1), h_c, start=True, stop=False)
                pe.wait_ge(msg_ready, c + 1)
                pe.matmul(r_acc[:], w(W_I), msg[:], start=False, stop=True).then_inc(r_acc_ready, 1)
                pe.matmul(in_acc[:], w(W_I + 2), msg[:], start=True, stop=True).then_inc(n_acc_ready, 1)
                pe.matmul(z_acc[:], w(W_I + 1), msg[:], start=False, stop=True).then_inc(z_acc_ready, 1)

            def body(c, first):
                for g in range(NG):
                    pe.wait_ge(loaded[g], 16 * c + 16)
                    if g == 0 and not first:
                        pe.wait_ge(agg_out, c)
                    for k in range(GR):
                        last = pe.matmul(acc[:], m.h[:, g * GR + k, :], a_in[:, g, k, :], start=(g + k == 0),
                                         stop=(g == NG - 1 and k == GR - 1))
                    last.then_inc(grouped, 1)
                if not first:
                    pe.wait_ge(h_out, c)
                gates(c)
            body(0, True)
            with pe.Fori(1, NCH) as c:
                body(c, False)

        @block.scalar
        def _(act):
            with act.Fori(0, NCH) as c:
                act.wait_ge(grouped, NG * c + NG)
                act.activation(agg[:], acc[:], ACT.Copy).then_inc(agg_out, 1)
                act.wait_ge(msg_acc_ready, c + 1)
                act.activation(msg[:], msg_acc[:], ACT.Relu, bias=m.b_msg[:]).then_inc(msg_ready, 1)
                act.wait_ge(r_acc_ready, c + 1)
                act.activation(r[:], r_acc[:], ACT.Sigmoid, bias=m.b_rz[:, 0:1]).then_inc(r_ready, 1)
                act.wait_ge(z_acc_ready, c + 1)
                act.activation(z[:], z_acc[:], ACT.Sigmoid, bias=m.b_rz[:, 1:2]).then_inc(z_ready, 1)
                act.wait_ge(n_sum_ready, c + 1)
                act.activation(new[:], n_in[:], ACT.Tanh, bias=m.b_ih[:, 2:3]).then_inc(n_ready, 1)

        @block.vector
        def _(dve):
            with dve.Fori(0, NCH) as c:
                step = Chain(dve, steps, c * 3)
                dve.wait_ge(r_ready, c + 1)
                step(dve.scalar_tensor_tensor(n_in[:], hn_acc[:], m.b_hh[:, 2:3], r[:], ALU.add, ALU.mult))
                dve.wait_ge(n_acc_ready, c + 1)
                dve.tensor_tensor(n_in[:], n_in[:], in_acc[:], ALU.add).then_inc(n_sum_ready, 1)
                dve.wait_ge(n_ready, c + 1)
                h_c = m.h_t[:, bass.ts(c, CW)]
                step(dve.tensor_tensor(diff[:], h_c, new[:], ALU.subtract))
                dve.wait_ge(z_ready, c + 1)
                step(dve.tensor_tensor(diff[:], diff[:], z[:], ALU.mult))
                dve.tensor_tensor(h_c, new[:], diff[:], ALU.add).then_inc(h_out, 1)


def layer2_end(nc, t, m, dram):
    with ExitStack() as ctx:
        sb = lambda name, shape, dt=F32: ctx.enter_context(nc.sbuf_tensor("le_" + name, shape, dt))
        sem = lambda name: ctx.enter_context(nc.semaphore("le_" + name))
        centred = sb("centred", [P, NB, D])
        square = sb("square", [P, NB, D])
        stat = sb("stat", [P, 6, NB])
        turned = ctx.enter_context(nc.psum_tensor("le_turned", [P, N], F32))
        turned_ready, var_ready, std_ready, h_ready, back, h_t_ready, projected, steps, g_out = (sem(n) for n in (
            "turned_ready", "var_ready", "std_ready", "h_ready", "back", "h_t_ready", "projected", "steps", "g_out"))
        block = ctx.enter_context(nc.Block())

        @block.tensor
        def _(pe):
            for b in range(NB):
                last = pe.transpose(turned[:, b * P:(b + 1) * P], m.h_t[:, b * P:(b + 1) * P], m.ident[:])
            last.then_inc(turned_ready, 1)
            pe.wait_ge(h_ready, 1)
            for c in range(NCH):
                for b in range(CB * c, CB * c + CB):
                    last = pe.transpose(turned[:, b * P:(b + 1) * P], m.h[:, b, :], m.ident[:])
                last.then_inc(back, 1)
            pe.wait_ge(h_t_ready, NCH)
            for b in range(NB):
                if b >= 16:
                    pe.wait_ge(g_out, b // 2 - 7)
                q = b % 16
                last = pe.matmul(turned[:, q * 2 * D:(q + 1) * 2 * D], m.h_t[:, b * P:(b + 1) * P], m.w_io[:], start=True, stop=True)
                if b % 2:
                    last.then_inc(projected, 1)

        @block.vector
        def _(dve):
            step = Chain(dve, steps)
            dve.wait_ge(turned_ready, 1)
            step(dve.tensor_tensor(m.x[:], m.x[:], turned[:].rearrange("p (b d) -> p b d", b=NB), ALU.add))
            normalise(step, dve, m.x[:], m.h[:], centred[:], square[:], stat, NB, var_ready, std_ready, 1).then_inc(h_ready, 1)
            for j in range(NB // 2):
                dve.wait_ge(projected, j + 1)
                q = j % 8
                both = turned[:, q * 4 * D:(q + 1) * 4 * D].rearrange("p (b k d) -> p k b d", b=2, k=2)
                dve.tensor_copy(m.h[:, 2 * j:2 * j + 2, :], both[:, 0])
                dve.tensor_copy(m.g[:, 2 * j:2 * j + 2, :], both[:, 1]).then_inc(g_out, 1)

        @block.scalar
        def _(act):
            root(act, stat, var_ready, std_ready, 1)
            for c in range(NCH):
                act.wait_ge(back, c + 1)
                act.activation(m.h_t[:, c * CW:(c + 1) * CW], turned[:, c * CW:(c + 1) * CW], ACT.Copy).then_inc(h_t_ready, 1)


def layer3(nc, t, m, dram):
    RING = 8
    with ExitStack() as ctx:
        sb = lambda name, shape, dt=F32: ctx.enter_context(nc.sbuf_tensor("l3_" + name, shape, dt))
        bank = lambda name, n=1: ctx.enter_context(nc.psum_tensor("l3_" + name, [P, n * CW], F32))
        sem = lambda name: ctx.enter_context(nc.semaphore("l3_" + name))
        a_in = sb("a_in", [P, RING, GR, CW])
        total = sb("total", [P, 2, CW])
        part = sb("part", [P, 2, CW])
        agg = sb("agg", [P, 2, CW])
        deg = sb("deg", [P, 3, 2, CB])
        out_c = sb("out_c", [P, CB, D])
        term = sb("term", [P, CB, D])
        acc = [bank(f"acc{k}") for k in range(2)]
        node = [bank(f"node{k}") for k in range(2)]
        degree = bank("degree")
        loaded = [sem(f"loaded{s}") for s in range(RING)]
        grouped, summed, agg_out, total_ready, deg_ready, node_ready, out_ready, stored, steps = (sem(n) for n in (
            "grouped", "summed", "agg_out", "total_ready", "deg_ready", "node_ready", "out_ready", "stored", "steps"))
        block = ctx.enter_context(nc.Block())
        sides = (dram.adj_t.rearrange("(g r p) m -> g p r m", r=GR, p=P), t["adj"].rearrange("(g r p) m -> g p r m", r=GR, p=P))
        out_rows = dram.out.rearrange("(c b p) d -> c p b d", b=CB, p=P)
        STEPS = 7

        @block.sync
        def _(sp):
            def body(c, first):
                for k in range(2):
                    for g in range(NG):
                        if not (first and k == 0):
                            at = NG * (2 * c + k - 1) + g + 1
                            wait_apart(sp, m.passed, grouped, at)
                            wait_apart(sp, m.passed, summed, at)
                        sp.dma_start(a_in[:, g], sides[k][g, :, :, bass.ts(c, CW)]).then_inc(loaded[g], 16)
                    if k == 0 and not first:
                        wait_apart(sp, m.passed, out_ready, c)
                        sp.dma_start(out_rows[bass.ts(c - 1, 1)].squeeze(0), out_c[:]).then_inc(stored, 16)
            body(0, True)
            with sp.Fori(1, NCH) as c:
                body(c, False)
            wait_apart(sp, m.passed, out_ready, NCH)
            sp.dma_start(out_rows[NCH - 1], out_c[:]).then_inc(stored, 16)
            sp.wait_ge(stored, 16 * NCH)

        @block.tensor
        def _(pe):
            def end(c):
                pe.wait_ge(total_ready, 2 * c + 2)
                for k in range(2):
                    for b in range(CB):
                        last = pe.matmul(degree[:, k * CB + b:k * CB + b + 1], total[:, k, b * P:(b + 1) * P], m.ones[:, 0:1], start=True, stop=True)
                last.then_inc(deg_ready, 1)
                for k in range(2):
                    pe.wait_ge(agg_out, 2 * c + k + 1)
                    for b in range(CB):
                        last = pe.transpose(node[k][:, b * P:(b + 1) * P], agg[:, k, b * P:(b + 1) * P], m.ident[:])
                    last.then_inc(node_ready, 1)

            def body(c, first):
                for k in range(2):
                    state = (m.h, m.g)[k]
                    for g in range(NG):
                        pe.wait_ge(loaded[g], 32 * c + 16 * k + 16)
                        if g == 0 and not first:
                            pe.wait_ge(agg_out, 2 * c - 1 + k)
                        for r in range(GR):
                            last = pe.matmul(acc[k][:], state[:, g * GR + r, :], a_in[:, g, r, :], start=(g + r == 0),
                                             stop=(g == NG - 1 and r == GR - 1))
                        last.then_inc(grouped, 1)
                if not first:
                    pe.wait_ge(out_ready, c)
                end(c)
            body(0, True)
            with pe.Fori(1, NCH) as c:
                body(c, False)

        @block.scalar
        def _(act):
            def body(c, first):
                for k in range(2):
                    act.wait_ge(grouped, NG * (2 * c + k) + NG)
                    if not first:
                        act.wait_ge(node_ready, 2 * c - 1 + k)
                    act.activation(agg[:, k, :], acc[k][:], ACT.Copy).then_inc(agg_out, 1)
            body(0, True)
            with act.Fori(1, NCH) as c:
                body(c, False)

        @block.vector
        def _(dve):
            def body(c, first):
                step = Chain(dve, steps, STEPS * c)
                for k in range(2):
                    for g in range(NG):
                        dve.wait_ge(loaded[g], 32 * c + 16 * k + 16)
                        if g == 0 and k == 0 and not first:
                            dve.wait_ge(deg_ready, c)
                        to = total[:, k, :] if g == 0 else part[:, g % 2, :]
                        dve.reduce_sum(to, a_in[:, g].rearrange("p r n -> p n r"), AX_X).then_inc(summed, 1)
                        dve.wait_ge(summed, NG * (2 * c + k) + g + 1)
                        if g:
                            add = dve.tensor_tensor(total[:, k, :], total[:, k, :], part[:, g % 2, :], ALU.add)
                    add.then_inc(total_ready, 1)
                dve.wait_ge(deg_ready, c + 1)
                some, safe, inverse = (deg[:, k] for k in range(3))
                both = degree[:, 0:2 * CB].rearrange("p (k b) -> p k b", k=2)
                step(dve.tensor_scalar(some, both, 0.0, None, ALU.is_gt))
                step(dve.tensor_tensor(safe, both, some, ALU.mult))
                step(dve.tensor_scalar(some, some, -1.0, 1.0, ALU.mult, ALU.add))
                step(dve.tensor_tensor(safe, safe, some, ALU.add))
                step(dve.reciprocal(inverse, safe))
                if not first:
                    dve.wait_ge(stored, 16 * c)
                dve.wait_ge(node_ready, 2 * c + 2)
                as_nodes = lambda v: v[:].rearrange("p (b d) -> p b d", b=CB)
                step(dve.tensor_tensor(out_c[:], as_nodes(node[0]), over(inverse[:, 0, :], CB), ALU.mult))
                dve.tensor_tensor(term[:], as_nodes(node[1]), over(inverse[:, 1, :], CB), ALU.mult)
                step(dve.tensor_tensor(out_c[:], out_c[:], m.x[:, bass.ts(c, CB), :], ALU.add))
                dve.tensor_tensor(out_c[:], out_c[:], term[:], ALU.add).then_inc(out_ready, 1)
            body(0, True)
            with dve.Fori(1, NCH) as c:
                body(c, False)


def graph_layers(nc, t, out, phases=(layer0, attention, layer1_end, layer2, layer2_end, layer3)):
    scratch = lambda name, shape: nc.dram_tensor(name, shape, F32, kind="Internal").ap()
    dram = Places()
    dram.adj_t, dram.out = scratch("adj_t", [N, N]), out
    dram.x1, dram.skip, dram.x2 = (scratch(name, [N, D]) for name in ("x1", "skip", "x2"))
    dram.q_stack, dram.k_stack = (scratch(name, [HEADS, P, N]) for name in ("q_stack", "k_stack"))
    with ExitStack() as ctx:
        sb = lambda name, shape, dt=F32: ctx.enter_context(nc.sbuf_tensor(name, shape, dt))
        m = Places()
        m.ident, m.ident_sum, m.ones = sb("ident", [P, P]), sb("ident_sum", [P, HC]), sb("ones", [P, 1])
        m.w_io, m.w_gru, m.w_beta = sb("w_io", [D, 2 * D]), sb("w_gru", [D, 7, D]), sb("w_beta", [P, 3 * D])
        m.b_msg = sb("b_msg", [D, 1])
        m.b_ih, m.b_hh, m.b_rz = sb("b_ih", [D, 3]), sb("b_hh", [D, 3]), sb("b_rz", [D, 2])
        m.col_inv = sb("col_inv", [P, NB])
        m.passed = ctx.enter_context(nc.semaphore("passed"))
        with ExitStack() as attention_only:
            asb = lambda name, shape, dt=F32: attention_only.enter_context(nc.sbuf_tensor(name, shape, dt))
            m.k_stack = asb("k_stack_sb", [P, HEADS, N], F32R)
            m.v = asb("v", [P, NB, D])
            for phase in phases[:2]:
                phase(nc, t, m, dram)
        m.h, m.x, m.g = (sb(name, [P, NB, D]) for name in ("h", "x", "g"))
        m.h_t = sb("later_h_t", [P, N])
        for phase in phases[2:]:
            phase(nc, t, m, dram)


_INS = ['x', 'adj', 'L1_gnn_Wq', 'L1_gnn_bq', 'L1_gnn_Wk', 'L1_gnn_bk', 'L1_gnn_Wv', 'L1_gnn_bv', 'L1_gnn_Ws',
        'L1_gnn_bs', 'L1_gnn_Wb', 'L2_gnn_W_msg', 'L2_gnn_b_msg', 'L2_gnn_W_ih', 'L2_gnn_W_hh', 'L2_gnn_b_ih',
        'L2_gnn_b_hh', 'L3_gnn_W_in', 'L3_gnn_W_out']


def kernel(**inputs):
    import numpy as np
    import concourse.bacc as bacc
    from concourse.bass_utils import run_bass_kernel_spmd

    nc = bacc.Bacc("TRN2", target_bir_lowering=False, num_devices=1)
    arrays, tensors = {}, {}
    for name in _INS:
        a = np.ascontiguousarray(inputs[name])
        arrays[name + "_in"] = a
        tensors[name] = nc.dram_tensor(name + "_in", a.shape, mybir.dt.from_np(a.dtype), kind="ExternalInput").ap()
    out = nc.dram_tensor("out", (N, D), F32, kind="ExternalOutput").ap()
    graph_layers(nc, tensors, out)
    return run_bass_kernel_spmd(nc, [arrays], core_ids=[0]).results[0]["out"]
```

```python
from contextlib import ExitStack

import concourse.bass as bass
from concourse import mybir

P = 128
N = 4096
D = 128
NB = N // P
CW = 512
NCH = N // CW
CB = CW // P
GR = 4
NG = NB // GR
HEADS = 4
HC = D // HEADS
SW = 1024
NS = N // SW
EPS = 1e-5
HIDE = -1.0e30
LOWEST = -3.0e38

F32 = mybir.dt.float32
F32R = mybir.dt.float32r
BF16 = mybir.dt.bfloat16
ALU = mybir.AluOpType
ACT = mybir.ActivationFunctionType
AX_X = mybir.AxisListType.X


class Places:
    pass


class Chain:

    def __init__(self, engine, sem, base=0):
        self.engine, self.sem, self.base, self.n = engine, sem, base, 0

    def __call__(self, instruction):
        self.n += 1
        instruction.then_inc(self.sem, 1)
        self.engine.wait_ge(self.sem, self.base + self.n)


def at(v, i):
    return v[i] if isinstance(i, int) else v[bass.ts(i, 1)].squeeze(0)


def wait_apart(engine, passed, sem, value):
    engine.wait_ge(sem, value)
    engine.sem_inc(passed, 1)


def over(stat, blocks):
    return stat.unsqueeze(2).to_broadcast([P, blocks, D])



def norm_mean(step, dve, x, stat, mean_ready):
    step(dve.reduce_sum(stat[:, 0, :], x, AX_X))
    dve.tensor_scalar(stat[:, 1, :], stat[:, 0, :], -1.0 / D, None, ALU.mult).then_inc(mean_ready, 1)


def norm_squares(act, x, unused, stat, blocks, mean_ready, squares_ready, turn):
    act.wait_ge(mean_ready, turn)
    for b in range(blocks):
        last = act.activation(unused[:, b, :], x[:, b, :], ACT.Square, bias=stat[:, 1, b:b + 1], accum_out=stat[:, 2, b:b + 1])
    last.then_inc(squares_ready, 1)


def norm_variance(dve, stat, squares_ready, var_ready, turn):
    dve.wait_ge(squares_ready, turn)
    dve.tensor_scalar(stat[:, 3, :], stat[:, 2, :], 1.0 / D, EPS, ALU.mult, ALU.add).then_inc(var_ready, 1)


def norm_root(act, stat, var_ready, std_ready, turn):
    act.wait_ge(var_ready, turn)
    act.activation(stat[:, 4, :], stat[:, 3, :], ACT.Sqrt).then_inc(std_ready, 1)


def norm_scale(step, dve, h, centred, stat, blocks, std_ready, turn):
    total, neg, square, var, std, inv = (stat[:, k, :] for k in range(6))
    dve.wait_ge(std_ready, turn)
    step(dve.reciprocal(inv, std))
    step(dve.scalar_tensor_tensor(total, inv, -0.5, var, ALU.mult, ALU.mult))
    step(dve.tensor_tensor(total, total, inv, ALU.mult))
    step(dve.scalar_tensor_tensor(inv, total, 1.5, inv, ALU.add, ALU.mult))
    return dve.scalar_tensor_tensor(h, centred, 0.0, over(inv, blocks), ALU.max, ALU.mult)


def normalise(step, dve, x, h, centred, stat, blocks, mean_ready, squares_ready, var_ready, std_ready, turn):
    norm_mean(step, dve, x, stat, mean_ready)
    dve.wait_ge(mean_ready, turn)
    step(dve.tensor_tensor(centred, x, over(stat[:, 1, :], blocks), ALU.add))
    norm_variance(dve, stat, squares_ready, var_ready, turn)
    return norm_scale(step, dve, h, centred, stat, blocks, std_ready, turn)


NORM_STEPS = 6


class FirstNorm:

    def __init__(self, ctx, nc, name, x, h_of):
        self.x, self.h_of = x, h_of
        self.stat = ctx.enter_context(nc.sbuf_tensor(name + "_stat", [P, 2, 6, CB], F32))
        self.centred = ctx.enter_context(nc.sbuf_tensor(name + "_centred", [P, 2, CB, D], F32))
        self.unused = ctx.enter_context(nc.sbuf_tensor(name + "_unused", [P, CB, D], BF16))
        self.x_loaded = [ctx.enter_context(nc.semaphore(f"{name}_x_loaded{g}")) for g in range(NG)]
        sem = lambda what: ctx.enter_context(nc.semaphore(name + "_" + what))
        self.mean_ready, self.squares_ready, self.centred_ready = sem("mean_ready"), sem("squares_ready"), sem("centred_ready")
        self.var_ready, self.std_ready, self.h_ready, self.steps = sem("var_ready"), sem("std_ready"), sem("h_ready"), sem("steps")

    def x_of(self, g):
        return self.x[:, g * CB:(g + 1) * CB, :]

    def begin(self, dve, step, g):
        dve.wait_ge(self.x_loaded[g], 16)
        norm_mean(step, dve, self.x_of(g), self.stat[:, g % 2], self.mean_ready)

    def centre(self, pool, g):
        pool.wait_ge(self.mean_ready, g + 1)
        if g >= 2:
            pool.wait_ge(self.h_ready, g - 1)
        pool.tensor_tensor(self.centred[:, g % 2], self.x_of(g), over(self.stat[:, g % 2, 1, :], CB), ALU.add)\
            .then_inc(self.centred_ready, 1)

    def squares(self, act, g):
        norm_squares(act, self.x_of(g), self.unused, self.stat[:, g % 2], CB, self.mean_ready, self.squares_ready, g + 1)

    def variance(self, dve, g):
        norm_variance(dve, self.stat[:, g % 2], self.squares_ready, self.var_ready, g + 1)

    def root(self, act, g):
        norm_root(act, self.stat[:, g % 2], self.var_ready, self.std_ready, g + 1)

    def finish(self, dve, step, g):
        dve.wait_ge(self.centred_ready, g + 1)
        norm_scale(step, dve, self.h_of(g), self.centred[:, g % 2], self.stat[:, g % 2], CB, self.std_ready, g + 1)\
            .then_inc(self.h_ready, 1)


def layer0(nc, t, m, dram):
    RING = 4
    with ExitStack() as ctx:
        sb = lambda name, shape, dt=F32: ctx.enter_context(nc.sbuf_tensor("l0_" + name, shape, dt))
        bank = lambda name, n=1: ctx.enter_context(nc.psum_tensor("l0_" + name, [P, n * CW], F32))
        sem = lambda name: ctx.enter_context(nc.semaphore("l0_" + name))
        w_q, w_k, w_vs = sb("w_q", [D, D]), sb("w_k", [D, D]), sb("w_vs", [D, 2 * D])
        b_q, b_k, b_vs = sb("b_q", [D, 1]), sb("b_k", [D, 1]), sb("b_vs", [P, 2 * D])
        x = sb("x", [P, NB, D])
        h0 = sb("h0", [P, NB, D])
        raw = sb("raw", [P, 7, D])
        a_in = sb("a_in", [P, RING, GR, CW])
        colsum = sb("colsum", [P, CW])
        part = sb("part", [P, 2, CW])
        row_part = sb("row_part", [P, NCH, NB])
        a_copy = sb("a_copy", [P, 2, GR, CW], BF16)
        msg_t = sb("msg_t", [P, CW])
        x1 = sb("x1", [P, CB, D])
        h_c = sb("h_c", [P, CB, D])
        centred = sb("centred", [P, CB, D])
        unused = sb("unused", [P, CB, D], BF16)
        h_t = sb("h_t", [P, CW])
        full = sb("full", [P, 2, CW])
        high = sb("high", [P, 2, CW], F32R)
        low = sb("low", [P, 2, CW], F32R)
        skip = sb("skip", [P, CB, D])
        stat = sb("stat", [P, 6, CB])
        deg = sb("deg", [P, 6, CB])
        row_deg = sb("row_deg", [P, 3, NB])
        acc = [bank(f"acc{k}") for k in range(2)]
        node = bank("node")
        proj = bank("proj", 2)
        turned = bank("turned", 2)
        first = FirstNorm(ctx, nc, "l0_first", x, lambda g: h0[:, g * CB:(g + 1) * CB, :])
        loaded = [sem(f"loaded{s}") for s in range(RING)]
        (w_loaded, zeroed, ident_ready, weights_turned, grouped, summed, rows_summed, added,
         deg_ready, msg_out, msg_turned, x1_ready, x1_stored, mean_ready, squares_ready, var_ready, std_ready, h_ready, h_turned,
         ht_ready, qk_ready, qk_split, qk_stored, k_loaded, vs_ready, vs_out, skip_stored, steps, row_steps) = (
            sem(n) for n in (
                "w_loaded", "zeroed", "ident_ready", "weights_turned",
                "grouped", "summed", "rows_summed", "added", "deg_ready", "msg_out", "msg_turned", "x1_ready",
                "x1_stored", "mean_ready", "squares_ready", "var_ready", "std_ready", "h_ready", "h_turned", "ht_ready", "qk_ready", "qk_split",
                "qk_stored", "k_loaded", "vs_ready", "vs_out", "skip_stored", "steps", "row_steps"))
        block = ctx.enter_context(nc.Block())
        a_rows = t["adj"].rearrange("(g r p) n -> g p r n", r=GR, p=P)
        x_groups = t["x"].rearrange("(g b p) d -> g p b d", b=CB, p=P)
        nodes = lambda v: v.rearrange("(c b p) d -> c p b d", b=CB, p=P)
        one_col = lambda v: v.rearrange("(p a) -> p a", a=1)
        weights = [
            (w_q[:], t["L1_gnn_Wq"]), (w_k[:], t["L1_gnn_Wk"]),
            (w_vs[:, 0:D], t["L1_gnn_Wv"]), (w_vs[:, D:2 * D], t["L1_gnn_Ws"]),
            (b_q[:], one_col(t["L1_gnn_bq"])), (b_k[:], one_col(t["L1_gnn_bk"])),
            (b_vs[:, 0:D], t["L1_gnn_bv"].partition_broadcast(P)), (b_vs[:, D:2 * D], t["L1_gnn_bs"].partition_broadcast(P)),
            (m.w_beta[:], t["L1_gnn_Wb"].rearrange("n o -> (n o)").partition_broadcast(P)),
            (raw[:, 0, :], t["L2_gnn_W_msg"]),
            (raw[:, 1:4, :], t["L2_gnn_W_ih"].rearrange("(g o) d -> o g d", g=3)),
            (raw[:, 4:7, :], t["L2_gnn_W_hh"].rearrange("(g o) d -> o g d", g=3)),
            (m.w_io[:, 0:D], t["L3_gnn_W_in"]), (m.w_io[:, D:2 * D], t["L3_gnn_W_out"]),
            (m.b_msg[:], one_col(t["L2_gnn_b_msg"])),
        ]
        for gate in range(3):
            rows = slice(gate * D, (gate + 1) * D)
            weights += [(m.b_ih[:, gate:gate + 1], one_col(t["L2_gnn_b_ih"][rows])),
                        (m.b_hh[:, gate:gate + 1], one_col(t["L2_gnn_b_hh"][rows]))]
        W_ALL = 16 * len(weights)
        K_STEPS = 9 + NORM_STEPS + 4

        def each(engine, body):
            body(0, 0, None, True)
            body(1, 1, 0, False)
            with engine.Fori(1, NCH // 2) as j:
                for k in range(2):
                    body(j * 2 + k, k, j * 2 + (k - 1), False)
            body(None, 0, NCH - 1, False)

        @block.sync
        def _(sp):
            def load(c, g):
                sp.dma_start(a_in[:, g % RING], a_rows[g, :, :, bass.ts(c, CW)]).then_inc(loaded[g % RING], 16)

            for g in range(NG):
                sp.dma_start(x[:, g * CB:(g + 1) * CB, :], x_groups[g]).then_inc(first.x_loaded[g], 16)
                if g < RING:
                    load(0, g)

            def reload(c, g):
                sp.wait_ge(grouped, NG * c + g - RING + 1)
                wait_apart(sp, m.passed, summed, NG * c + g - RING + 1)
                wait_apart(sp, m.passed, rows_summed, NG * c + g - RING + 1)
                load(c, g)

            for g in range(RING, NG):
                reload(0, g)
            with sp.Fori(1, NCH) as c:
                for g in range(NG):
                    reload(c, g)

        @block.tensor
        def _(pe):
            def stream(c, k, g, opening):
                pe.wait_ge(loaded[g % RING], 16 * (NG // RING) * c + 16 * (g // RING) + 16)
                if opening:
                    pe.wait_ge(first.h_ready, g + 1)
                if g == 0 and not (isinstance(c, int) and c < 2):
                    pe.wait_ge(msg_out, c - 1)
                for r in range(GR):
                    last = pe.matmul(acc[k][:], h0[:, GR * g + r, :], a_in[:, g % RING, r, :],
                                     start=(g == 0 and r == 0), stop=(g == NG - 1 and r == GR - 1))
                last.then_inc(grouped, 1)

            def turn_weights():
                pe.wait_ge(w_loaded, W_ALL)
                for k in range(7):
                    last = pe.transpose(turned[:, k * P:(k + 1) * P], raw[:, k, :], m.ident[:])
                last.then_inc(weights_turned, 1)

            def degrees_and_message(e, later):
                pe.wait_ge(added, NG * e + NG)
                if later:
                    pe.wait_ge(vs_out, e)
                for b in range(CB):
                    last = pe.matmul(proj[:, b:b + 1], colsum[:, b * P:(b + 1) * P], m.ones[:, 0:1], start=True, stop=True)
                last.then_inc(deg_ready, 1)
                pe.wait_ge(msg_out, e + 1)
                for b in range(CB):
                    last = pe.transpose(node[:, b * P:(b + 1) * P], msg_t[:, b * P:(b + 1) * P], m.ident[:])
                last.then_inc(msg_turned, 1)

            def turn_h(e):
                pe.wait_ge(h_ready, e + 1)
                for b in range(CB):
                    last = pe.transpose(node[:, b * P:(b + 1) * P], h_c[:, b, :], m.ident[:])
                last.then_inc(h_turned, 1)

            def project_qk(e):
                pe.wait_ge(ht_ready, e + 1)
                pe.matmul(proj[:, 0:CW], w_q[:], h_t[:], start=True, stop=True).then_inc(qk_ready, 1)
                pe.matmul(proj[:, CW:2 * CW], w_k[:], h_t[:], start=True, stop=True).then_inc(qk_ready, 1)

            def project_vs(e):
                pe.wait_ge(qk_split, 2 * e + 2)
                for b in range(CB):
                    last = pe.matmul(proj[:, b * 2 * D:(b + 1) * 2 * D], h_t[:, b * P:(b + 1) * P], w_vs[:],
                                     start=True, stop=True)
                last.then_inc(vs_ready, 1)

            def body(c, k, e, opening):
                for g in range(NG):
                    if c is not None:
                        stream(c, k, g, opening)
                    if e is not None:
                        if g == 0:
                            degrees_and_message(e, c is None or not isinstance(c, int))
                        elif g == 3:
                            turn_h(e)
                        elif g == 4:
                            project_qk(e)
                        elif g == 6:
                            project_vs(e)
                if opening:
                    turn_weights()

            pe.wait_ge(ident_ready, 1)
            each(pe, body)

        @block.scalar
        def _(act):
            def copy_message(c, k):
                act.wait_ge(grouped, NG * c + NG)
                act.activation(msg_t[:], acc[k][:], ACT.Copy).then_inc(msg_out, 1)

            def chunk_of(c):
                return row_part[:, bass.ts(c, 1), :].squeeze(1)

            def sum_rows(c, g):
                act.wait_ge(loaded[g % RING], 16 * (NG // RING) * c + 16 * (g // RING) + 16)
                if not (isinstance(c, int) and c == 0 and g < 2):
                    act.wait_ge(rows_summed, NG * c + g - 1)
                act.sem_inc(m.passed, 1)
                for r in range(GR):
                    last = act.activation(a_copy[:, g % 2, r, :], a_in[:, g % RING, r, :], ACT.Copy,
                                          accum_out=chunk_of(c)[:, GR * g + r:GR * g + r + 1])
                last.then_inc(rows_summed, 1)

            def behind(g, e):
                if g == 1:
                    norm_squares(act, x1, unused, stat, CB, mean_ready, squares_ready, e + 1)
                    norm_root(act, stat, var_ready, std_ready, e + 1)
                    act.wait_ge(x1_ready, e + 1)
                    act.dma_start(at(nodes(dram.x1), e), x1[:]).then_inc(x1_stored, 16)
                elif g == 3:
                    act.wait_ge(h_turned, e + 1)
                    act.activation(h_t[:], node[:], ACT.Copy).then_inc(ht_ready, 1)
                elif g == 6:
                    for k, parts in enumerate((dram.q_parts, dram.k_parts)):
                        act.wait_ge(qk_split, 2 * e + k + 1)
                        for s, half in enumerate((high, low)):
                            to = parts[:, s * HC:(s + 1) * HC, bass.ts(e, CW)]
                            act.dma_start(to, half[:, k, :].bitcast(F32)).then_inc(qk_stored, 16)
                elif g == 7:
                    act.wait_ge(vs_out, e + 1)
                    act.dma_start(at(nodes(dram.skip), e), skip[:]).then_inc(skip_stored, 16)

            def fetch_k(e):
                act.wait_ge(qk_stored, 64 * e + 64)
                for s in range(4):
                    of = dram.k_parts[:, s // 2 * HC:(s // 2 + 1) * HC, bass.ts(e, CW)]
                    act.dma_start(m.k_stack[s * HC:(s + 1) * HC, :, bass.ts(e, CW)].bitcast(F32),
                                  of.rearrange("h s n -> s h n")).then_inc(k_loaded, 16)

            first.squares(act, 0)
            first.root(act, 0)
            def body(c, k, e, opening):
                for g in range(NG):
                    if opening:
                        if g < NG - 1:
                            first.squares(act, g + 1)
                        for to, of in weights[g * 3:(g + 1) * 3] if g < NG - 1 else weights[g * 3:]:
                            act.dma_start(to, of).then_inc(w_loaded, 16)
                    if c is not None:
                        sum_rows(c, g)
                    if opening and g < NG - 1:
                        first.root(act, g + 1)
                    if e is not None:
                        behind(g, e)
                if c is not None:
                    copy_message(c, k)
                if opening:
                    act.wait_ge(weights_turned, 1)
                    act.activation(m.w_gru[:], turned[:, 0:7 * P].rearrange("p (k o) -> p k o", k=7), ACT.Copy)
                else:
                    fetch_k(e)

            each(act, body)
            for stored, n in ((x1_stored, 16), (skip_stored, 16), (k_loaded, 64)):
                act.wait_ge(stored, n * NCH)

        @block.vector
        def _(dve):
            def stream(c, g, opening):
                dve.wait_ge(loaded[g % RING], 16 * (NG // RING) * c + 16 * (g // RING) + 16)
                if not (opening and g < 2):
                    dve.wait_ge(added, NG * c + g - 1)
                dve.reduce_sum(part[:, g % 2, :], a_in[:, g % RING].rearrange("p r n -> p n r"), AX_X).then_inc(summed, 1)

            def add_message(e, step, later):
                dve.wait_ge(deg_ready, e + 1)
                empty, safe, inverse, some, safe3 = (deg[:, k, :] for k in range(5))
                total = proj[:, 0:CB]
                step(dve.tensor_scalar(empty, total, 0.0, None, ALU.is_equal))
                step(dve.tensor_tensor(safe, total, empty, ALU.add))
                step(dve.reciprocal(inverse, safe))
                step(dve.tensor_scalar(empty, empty, -1.0, 1.0, ALU.mult, ALU.add))
                step(dve.tensor_tensor(inverse, inverse, empty, ALU.mult))
                step(dve.tensor_scalar(some, total, 0.0, None, ALU.is_gt))
                dve.tensor_tensor(safe3, total, some, ALU.mult)
                step(dve.tensor_scalar(some, some, -1.0, 1.0, ALU.mult, ALU.add))
                step(dve.tensor_tensor(safe3, safe3, some, ALU.add))
                dve.reciprocal(m.col_inv[:, bass.ts(e, CB)], safe3)
                dve.wait_ge(msg_turned, e + 1)
                if later:
                    dve.wait_ge(x1_stored, 16 * e)
                step(dve.tensor_tensor(h_c[:], node[:].rearrange("p (b d) -> p b d", b=CB), over(inverse, CB), ALU.mult))
                dve.tensor_tensor(x1[:], x[:, bass.ts(e, CB), :], h_c[:], ALU.add).then_inc(x1_ready, 1)
                dve.wait_ge(x1_ready, e + 1)
                normalise(step, dve, x1[:], h_c[:], centred[:], stat, CB, mean_ready, squares_ready, var_ready, std_ready, e + 1)\
                    .then_inc(h_ready, 1)

            def split_qk(e, step, later):
                if later:
                    dve.wait_ge(qk_stored, 64 * e)
                for k in range(2):
                    dve.wait_ge(qk_ready, 2 * e + k + 1)
                    if k == 0:
                        step(dve.tensor_scalar(full[:, 0, :], proj[:, 0:CW], b_q[:], float(HC) ** -0.5, ALU.add, ALU.mult))
                    else:
                        step(dve.tensor_scalar(full[:, 1, :], proj[:, CW:2 * CW], b_k[:], None, ALU.add))
                    step(dve.tensor_copy(high[:, k, :], full[:, k, :]))
                    dve.tensor_tensor(low[:, k, :], full[:, k, :], high[:, k, :].bitcast(F32), ALU.subtract).then_inc(qk_split, 1)

            def add_vs(e, later):
                dve.wait_ge(vs_ready, e + 1)
                if later:
                    dve.wait_ge(skip_stored, 16 * e)
                vs = proj[:].rearrange("p (b k d) -> p b k d", b=CB, k=2)
                bias = lambda k: b_vs[:, k * D:(k + 1) * D].unsqueeze(1).to_broadcast([P, CB, D])
                dve.tensor_tensor(m.v[:, bass.ts(e, CB), :], vs[:, :, 0, :], bias(0), ALU.add)
                dve.tensor_tensor(skip[:], vs[:, :, 1, :], bias(1), ALU.add).then_inc(vs_out, 1)

            def body(c, k, e, opening):
                later = e is not None and not (isinstance(e, int) and e == 0)
                step = Chain(dve, first.steps) if opening else Chain(dve, steps, K_STEPS * e)
                if opening:
                    first.begin(dve, step, 0)
                    first.variance(dve, 0)
                for g in range(NG):
                    if opening:
                        if g < NG - 1:
                            first.begin(dve, step, g + 1)
                        first.finish(dve, step, g)
                    if c is not None:
                        stream(c, g, opening)
                    if opening and g < NG - 1:
                        first.variance(dve, g + 1)
                    if e is not None:
                        if g == 1:
                            add_message(e, step, later)
                        elif g == 4:
                            split_qk(e, step, later)
                        elif g == 7:
                            add_vs(e, later)
                assert opening or step.n == K_STEPS, step.n
                if opening:
                    dve.wait_ge(w_loaded, W_ALL)
                    dve.tensor_tensor(m.b_rz[:], m.b_ih[:, 0:2], m.b_hh[:, 0:2], ALU.add)

            each(dve, body)
            step = Chain(dve, row_steps)
            total, some, safe = (row_deg[:, k, :] for k in range(3))
            dve.wait_ge(rows_summed, NG * NCH)
            step(dve.reduce_sum(total, row_part[:].rearrange("p c b -> p b c"), AX_X))
            step(dve.tensor_scalar(some, total, 0.0, None, ALU.is_gt))
            step(dve.tensor_tensor(safe, total, some, ALU.mult))
            step(dve.tensor_scalar(some, some, -1.0, 1.0, ALU.mult, ALU.add))
            step(dve.tensor_tensor(safe, safe, some, ALU.add))
            dve.reciprocal(m.row_inv[:], safe)

        @block.gpsimd
        def _(pool):
            pool.memset(m.ident[:], 0.0).then_inc(zeroed, 1)
            pool.memset(m.ones[:], 1.0)
            pool.wait_ge(zeroed, 1)
            pool.affine_select(out=m.ident[:], in_=m.ident[:], compare_op=ALU.not_equal, fill=1.0, base=0,
                               pattern=[[-1, P]], channel_multiplier=1).then_inc(ident_ready, 1)
            pool.wait_ge(ident_ready, 1)
            pool.tensor_tensor(m.ident_sum[:], m.ident[:, 0:HC], m.ident[:, HC:2 * HC], ALU.add).then_inc(zeroed, 1)
            for k in range(2, 4):
                pool.wait_ge(zeroed, k)
                pool.tensor_tensor(m.ident_sum[:], m.ident_sum[:], m.ident[:, k * HC:(k + 1) * HC], ALU.add).then_inc(zeroed, 1)

            def body(c, opening):
                for g in range(NG):
                    if opening and g < NG - 1:
                        first.centre(pool, g + 1)
                    if g == 0 and not opening:
                        pool.wait_ge(deg_ready, c)
                    wait_apart(pool, m.passed, summed, NG * c + g + 1)
                    if g == 0:
                        pool.tensor_copy(colsum[:], part[:, 0, :]).then_inc(added, 1)
                    else:
                        pool.wait_ge(added, NG * c + g)
                        pool.tensor_tensor(colsum[:], colsum[:], part[:, g % 2, :], ALU.add).then_inc(added, 1)

            first.centre(pool, 0)
            body(0, True)
            with pool.Fori(1, NCH) as c:
                body(c, False)


def attention(nc, t, m, dram):
    UNITS = HEADS * NB
    LEAD = 2
    GC = 4
    G = NB // GC
    PARTS = N // CW
    BY_DVE = (1, 7)
    with ExitStack() as ctx:
        sb = lambda name, shape, dt=F32: ctx.enter_context(nc.sbuf_tensor("at_" + name, shape, dt))
        bank = lambda name, n=1: ctx.enter_context(nc.psum_tensor("at_" + name, [P, n * CW], F32))
        sem = lambda name: ctx.enter_context(nc.semaphore("at_" + name))
        a_in = sb("a_in", [P, N])
        mask = sb("mask", [P, 2, N], BF16)
        q_in = sb("q_in", [P, HEADS, P], F32R)
        probs = sb("probs", [P, HEADS, N])
        stage = sb("stage", [P, 2, 2 * GC, P])
        top = sb("top", [P, HEADS, PARTS])
        neg = sb("neg", [P, 2, HEADS])
        sums = sb("sums", [P, HEADS, NS])
        total = sb("total", [P, 3])
        tiles = sb("tiles", [P, 2, P])
        both = sb("both", [P, 2, 3, D])
        x = sb("x", [P, 2, D])
        product = sb("product", [P, 3 * D], BF16)
        gate = sb("gate", [P, 5])
        scores = [bank(f"scores{k}") for k in range(2)]
        turned = [bank(f"turned{k}") for k in range(4)]
        value = [bank(f"value{k}") for k in range(2)]
        a_loaded = [sem(f"a_loaded{c}") for c in range(NS)]
        q_loaded = [sem(f"q_loaded{h}") for h in range(HEADS)]
        x_loaded = [sem(f"x_loaded{k}") for k in range(2)]
        x_stored = [sem(f"x_stored{k}") for k in range(2)]
        stage_stored = [sem(f"stage_stored{k}") for k in range(2)]
        (a_turned, a_dve, a_act, logit_ready, gate_ready, x2_ready, gate_steps, first_mask, mask_ready, scores_ready,
         masked, max_ready, bias_ready, exp_ready, transposed, act_copied, dve_copied, tiled, tiles_out, summed,
         out_ready, steps) = (sem(n) for n in (
             "a_turned", "a_dve", "a_act", "logit_ready", "gate_ready", "x2_ready", "gate_steps", "first_mask",
             "mask_ready", "scores_ready", "masked", "max_ready", "bias_ready", "exp_ready", "transposed",
             "act_copied", "dve_copied", "tiled", "tiles_out", "summed", "out_ready", "steps"))
        block = ctx.enter_context(nc.Block())
        a_rows = t["adj"].rearrange("(b p) n -> b p n", p=P)
        blocks = lambda v: v.rearrange("(b p) d -> b p d", p=P)
        at_rows = dram.adj_t.rearrange("(h j p) n -> h p j n", j=2 * GC, p=P)

        def bank_of(h, s):
            return turned[(s + 2 * (h % 2)) % 4]

        def bank_of_group(h, g):
            return bank_of(h, g if g < 4 else g + 2)

        def wait_copied(engine, u, g):
            if g < 0:
                u, g = u - 1, g + G
            mine = sum(k <= g for k in BY_DVE)
            if g in BY_DVE:
                engine.wait_ge(dve_copied, len(BY_DVE) * u + mine)
            else:
                engine.wait_ge(act_copied, (G - len(BY_DVE)) * u + g + 1 - mine)

        @block.sync
        def _(sp):
            def load_a(i, h, first=False):
                if not first:
                    wait_apart(sp, m.passed, a_turned, 2 * (HEADS * (i - 1) + h) + 2)
                    if isinstance(i, int) and i == 1:
                        wait_apart(sp, m.passed, first_mask, h + 1)
                    else:
                        wait_apart(sp, m.passed, mask_ready, NS * (i - 2) + h + 1)
                sp.dma_start(a_in[:, h * SW:(h + 1) * SW], at(a_rows, i)[:, h * SW:(h + 1) * SW]).then_inc(a_loaded[h], 16)

            def load_q(i, h, first=False):
                if not first:
                    wait_apart(sp, m.passed, scores_ready, PARTS * (HEADS * (i - 1) + h) + PARTS)
                for half in range(2):
                    sp.dma_start(q_in[half * 2 * HC:(half + 1) * 2 * HC, h, :].bitcast(F32),
                                 dram.q_parts[h, :, bass.ts(i, P)]).then_inc(q_loaded[h], 16)

            def store_stage(i, h):
                wait_apart(sp, m.passed, a_dve, HEADS * i + h + 1)
                wait_apart(sp, m.passed, a_act, HEADS * i + h + 1)
                sp.dma_start(at_rows[h, :, :, bass.ts(i, P)], stage[:, h % 2]).then_inc(stage_stored[h % 2], 16)

            def load_x(i, k, first=False):
                if not first:
                    wait_apart(sp, m.passed, x_stored[k], 8 * (i - k))
                sp.dma_start(both[:, k, 1, :], at(blocks(dram.skip), i)).then_inc(x_loaded[k], 16)
                sp.dma_start(x[:, k, :], at(blocks(dram.x1), i)).then_inc(x_loaded[k], 16)

            def store_x(i, k):
                wait_apart(sp, m.passed, x2_ready, i + 1)
                sp.dma_start(at(blocks(dram.x2), i), x[:, k, :]).then_inc(x_stored[k], 16)

            def period(i, k):
                for h in range(HEADS):
                    if not (isinstance(i, int) and i == NB - 1):
                        load_q(i + 1, h)
                        store_stage(i + 1, h)
                    if not (isinstance(i, int) and i >= NB - 2):
                        load_a(i + 2, h)
                    if h == 3 and not (isinstance(i, int) and i == 0):
                        store_x(i - 1, 1 - k)
                    if h == 3 and not (isinstance(i, int) and i == NB - 1):
                        load_x(i + 1, 1 - k, isinstance(i, int) and i == 0)

            for h in range(HEADS):
                load_q(0, h, True)
                load_a(0, h, True)
            load_x(0, 0, True)
            for h in range(HEADS):
                store_stage(0, h)
                load_a(1, h)
            for i in range(2):
                period(i, i)
            with sp.Fori(1, NB // 2 - 1) as j:
                for k in range(2):
                    period(j * 2 + k, k)
            for i in (NB - 2, NB - 1):
                period(i, i % 2)
            store_x(NB - 1, 1)
            for k in range(2):
                sp.wait_ge(x_stored[k], 16 * (NB // 2))
                sp.wait_ge(stage_stored[k], 16 * (NB * HEADS // 2))

        @block.gpsimd
        def _(pool):
            def make(i, k, first=False):
                for c in range(NS):
                    if c == 0 and not first:
                        pool.wait_ge(masked, PARTS * HEADS * (i - 1))
                    wait_apart(pool, m.passed, a_loaded[c], 16 * i + 16)
                    pool.tensor_scalar(mask[:, k, c * SW:(c + 1) * SW], a_in[:, c * SW:(c + 1) * SW], 0.0, HIDE,
                                       ALU.is_equal, ALU.mult).then_inc(mask_ready, 1)

            make(1, 1, True)
            with pool.Fori(1, NB // 2) as j:
                for k in range(2):
                    make(j * 2 + k, k)

        @block.tensor
        def _(pe):
            def score(u, h, i, p, first=False):
                if p == 0:
                    pe.wait_ge(q_loaded[h], 32 * i + 32)
                if not (first and p < 2):
                    pe.wait_ge(masked, PARTS * u + p - 1)
                pe.matmul(scores[p % 2][:], q_in[:, h, :], m.k_stack[:, h, p * CW:(p + 1) * CW],
                          start=True, stop=True).then_inc(scores_ready, 1)

            def values(u, h, g):
                if g < 0:
                    u, h, g = u - 1, (h - 1) % HEADS, g + G
                if g == 0 and not (isinstance(u, int) and u < 2):
                    pe.wait_ge(out_ready, u - 1)
                for r in range(GC):
                    part = slice((g * GC + r) * P, (g * GC + r + 1) * P)
                    last = pe.matmul(value[h % 2][r * HC:(r + 1) * HC, 0:P], m.v[:, g * GC + r, h * HC:(h + 1) * HC],
                                     probs[:, h, part], start=(g == 0), stop=(g == G - 1))
                if g == G - 1:
                    last.then_inc(tiled, 1)

            def add_tiles(u, k):
                pe.wait_ge(tiles_out, u + 1)
                pe.matmul(value[k][:, P:P + HC], tiles[:, k, :], m.ident_sum[:], start=True, stop=True).then_inc(summed, 1)

            def turn_a(i, h, first=False):
                pe.wait_ge(a_loaded[h], 16 * i + 16)
                for half in range(2):
                    if first and h >= 2:
                        pe.wait_ge((a_dve, a_act)[half], h - 1)
                    to = bank_of(h, 4 + half)
                    for r in range(GC):
                        col = h * SW + (half * GC + r) * P
                        last = pe.transpose(to[:, r * P:(r + 1) * P], a_in[:, col:col + P], m.ident[:])
                    last.then_inc(a_turned, 1)

            def turn(u, h, g):
                to = bank_of_group(h, g)
                for r in range(GC):
                    last = pe.transpose(to[:, r * P:(r + 1) * P],
                                        probs[:, h, (g * GC + r) * P:(g * GC + r + 1) * P], m.ident[:])
                last.then_inc(transposed, 1)

            def unit(i, h, first=False, last=False):
                u = i * HEADS + h
                begun = not (first and h == 0)
                scored = not (last and h >= HEADS - LEAD)
                ahead = lambda p: score(u + LEAD, (h + LEAD) % HEADS, i + (h + LEAD) // HEADS, p)
                for g in range(0, G, 2):
                    if scored:
                        ahead(g)
                    if g == 4:
                        wait_copied(pe, u, 0)
                        wait_copied(pe, u, 1)
                        if not last:
                            turn_a(i + 1, h)
                    pe.wait_ge(exp_ready, NS * u + g // 2 + 1)
                    for k in range(2):
                        if g < 4 and begun:
                            wait_copied(pe, u, g + k - 4)
                        elif g < 4:
                            pe.wait_ge((a_dve, a_act)[k], 3 + g // 2)
                        elif g == 4:
                            wait_copied(pe, u, 2 + k)
                        elif not last:
                            pe.wait_ge((a_dve, a_act)[k], u + HEADS + 1)
                        turn(u, h, g + k)
                    if g == 6 and begun:
                        add_tiles(u - 1, (h - 1) % 2)
                    if scored:
                        ahead(g + 1)
                    if begun or g >= 4:
                        values(u, h, g - 4)
                        values(u, h, g - 3)

            for c in range(NS):
                turn_a(0, c, first=True)
                for p in (2 * c, 2 * c + 1):
                    score(0, 0, 0, p, first=True)
            for p in range(PARTS):
                score(1, 1, 0, p)
            for h in range(HEADS):
                unit(0, h, first=True)
            with pe.Fori(1, NB - 1) as i:
                for h in range(HEADS):
                    unit(i, h)
            for h in range(HEADS):
                unit(NB - 1, h, last=True)
            for g in range(G - 4, G):
                wait_copied(pe, UNITS - 1, g)
                values(UNITS - 1, HEADS - 1, g)
            add_tiles(UNITS - 1, 1)

        @block.scalar
        def _(act):
            def exponentials(u, h, c):
                if c == 0:
                    act.wait_ge(bias_ready, u + 1)
                act.activation(probs[:, h, c * SW:(c + 1) * SW], probs[:, h, c * SW:(c + 1) * SW], ACT.Exp,
                               bias=neg[:, 1, h:h + 1], accum_out=sums[:, h, c:c + 1]).then_inc(exp_ready, 1)

            def copy_a(i, h, first=False):
                act.wait_ge(a_turned, 2 * (HEADS * i + h) + 2)
                if not (first and h < 2):
                    act.wait_ge(stage_stored[h % 2], 16 * (2 * i + h // 2))
                act.activation(stage[:, h % 2, GC:, :], bank_of(h, 5)[:].rearrange("p (j n) -> p j n", n=P), ACT.Copy)\
                    .then_inc(a_act, 1)

            def exp_of_gate(i):
                act.wait_ge(logit_ready, i + 1)
                act.activation(gate[:, 2:3], gate[:, 1:2], ACT.Exp, scale=-1.0).then_inc(gate_ready, 1)

            def tiles_of(u, k):
                act.wait_ge(tiled, u + 1)
                act.activation(tiles[:, k, :], value[k][:, 0:P], ACT.Copy).then_inc(tiles_out, 1)

            def unit(i, h, first=False, last=False):
                u = i * HEADS + h
                for c in range(NS):
                    for g in (2 * c, 2 * c + 1):
                        if g not in BY_DVE:
                            act.wait_ge(transposed, G * u + g + 1)
                            act.activation(probs[:, h, g * CW:(g + 1) * CW], bank_of_group(h, g)[:], ACT.Copy)\
                                .then_inc(act_copied, 1)
                    if not (last and h == HEADS - 1):
                        exponentials(u + 1, (h + 1) % HEADS, c)
                    if c == 1 and not (first and h == 0):
                        tiles_of(u - 1, (h - 1) % 2)
                    if c == 1 and not last:
                        copy_a(i + 1, h)
                    if c == 3 and h == 2 and not first:
                        exp_of_gate(i - 1)

            for h in range(HEADS):
                copy_a(0, h, first=True)
            for c in range(NS):
                exponentials(0, 0, c)
            for h in range(HEADS):
                unit(0, h, first=True)
            with act.Fori(1, NB - 1) as i:
                for h in range(HEADS):
                    unit(i, h)
            for h in range(HEADS):
                unit(NB - 1, h, last=True)
            tiles_of(UNITS - 1, 1)
            exp_of_gate(NB - 1)

        @block.vector
        def _(dve):
            def mask_part(u, h, i, k, p):
                if h == 0 and p % 2 == 0 and not (isinstance(i, int) and i == 0):
                    dve.wait_ge(mask_ready, NS * (i - 1) + p // 2 + 1)
                wait_apart(dve, m.passed, scores_ready, PARTS * u + p + 1)
                part = slice(p * CW, (p + 1) * CW)
                dve.tensor_tensor_reduce(
                    out=probs[:, h, part], in0=scores[p % 2][:], in1=mask[:, k, part],
                    scale=1.0, scalar=LOWEST, op0=ALU.add, op1=ALU.max, accum_out=top[:, h, p:p + 1]).then_inc(masked, 1)

            def maximum(u, h):
                dve.wait_ge(masked, PARTS * u + PARTS)
                dve.tensor_reduce(neg[:, 0, h:h + 1], top[:, h, :], AX_X, ALU.max, negate=True).then_inc(max_ready, 1)

            def bias_of(u, h):
                dve.wait_ge(max_ready, u + 1)
                dve.scalar_tensor_tensor(neg[:, 1, h:h + 1], neg[:, 0, h:h + 1], -HIDE / 2, neg[:, 0, h:h + 1],
                                         ALU.is_lt, ALU.mult).then_inc(bias_ready, 1)

            def copy_out(u, h, g):
                dve.wait_ge(transposed, G * u + g + 1)
                dve.tensor_copy(probs[:, h, g * CW:(g + 1) * CW], bank_of_group(h, g)[:]).then_inc(dve_copied, 1)

            def copy_a(i, h, first=False):
                dve.wait_ge(a_turned, 2 * (HEADS * i + h) + 1)
                if not (first and h < 2):
                    dve.wait_ge(stage_stored[h % 2], 16 * (2 * i + h // 2))
                dve.tensor_copy(stage[:, h % 2, 0:GC, :], bank_of(h, 4)[:].rearrange("p (j n) -> p j n", n=P)).then_inc(a_dve, 1)

            def gate_steps_of(i, k):
                done = 5 * i

                def difference():
                    dve.wait_ge(out_ready, HEADS * i + HEADS)
                    dve.wait_ge(x_loaded[k], 16 * (i - k) + 32)
                    dve.tensor_tensor(both[:, k, 2, :], both[:, k, 0, :], both[:, k, 1, :], ALU.subtract).then_inc(gate_steps, 1)

                def logit():
                    dve.wait_ge(gate_steps, done + 1)
                    dve.tensor_tensor_reduce(out=product[:], in0=both[:, k].rearrange("p k d -> p (k d)"), in1=m.w_beta[:],
                                             scale=1.0, scalar=0.0, op0=ALU.mult, op1=ALU.add,
                                             accum_out=gate[:, 0:1]).then_inc(gate_steps, 1)

                def bound():
                    dve.wait_ge(gate_steps, done + 2)
                    dve.tensor_scalar(gate[:, 1:2], gate[:, 0:1], -80.0, None, ALU.max).then_inc(logit_ready, 1)

                def one_more():
                    dve.wait_ge(gate_ready, i + 1)
                    dve.tensor_scalar(gate[:, 3:4], gate[:, 2:3], 1.0, None, ALU.add).then_inc(gate_steps, 1)

                def beta():
                    dve.wait_ge(gate_steps, done + 3)
                    dve.reciprocal(gate[:, 4:5], gate[:, 3:4]).then_inc(gate_steps, 1)

                def scaled():
                    dve.wait_ge(gate_steps, done + 4)
                    dve.tensor_tensor(x[:, k, :], x[:, k, :], both[:, k, 0, :], ALU.add)
                    dve.tensor_scalar(both[:, k, 2, :], both[:, k, 2, :], gate[:, 4:5], None, ALU.mult).then_inc(gate_steps, 1)

                def finish():
                    dve.wait_ge(gate_steps, done + 5)
                    dve.tensor_tensor(x[:, k, :], x[:, k, :], both[:, k, 2, :], ALU.subtract).then_inc(x2_ready, 1)

                return difference, logit, bound, one_more, beta, scaled, finish

            def head_steps_of(u, h, k):
                done = 3 * u

                def sum_up():
                    dve.wait_ge(exp_ready, NS * u + NS)
                    dve.reduce_sum(total[:, 0:1], sums[:, h, :], AX_X).then_inc(steps, 1)

                def safe():
                    dve.wait_ge(steps, done + 1)
                    dve.scalar_tensor_tensor(total[:, 1:2], total[:, 0:1], 0.0, total[:, 0:1], ALU.is_equal, ALU.add)\
                        .then_inc(steps, 1)

                def invert():
                    dve.wait_ge(steps, done + 2)
                    dve.reciprocal(total[:, 2:3], total[:, 1:2]).then_inc(steps, 1)

                def scale():
                    dve.wait_ge(steps, done + 3)
                    dve.wait_ge(summed, u + 1)
                    result = both[:, k, 0, :].rearrange("p (c h) -> p c h", h=HEADS)
                    dve.tensor_scalar(result[:, :, h], value[h % 2][:, P:P + HC], total[:, 2:3], None, ALU.mult)\
                        .then_inc(out_ready, 1)

                return sum_up, safe, invert, scale

            def unit(i, h, k, first=False, last=False):
                u = i * HEADS + h
                after = h + LEAD
                if not (first and h == 0):
                    sum_up, safe, invert, scale = head_steps_of(u - 1, (h - 1) % HEADS, k if h else 1 - k)
                if not first:
                    difference, logit, bound, one_more, beta, scaled, finish = gate_steps_of(i - 1, 1 - k)
                for g in range(G):
                    if not (last and after >= HEADS):
                        mask_part(u + LEAD, after % HEADS, i + after // HEADS, (k + after // HEADS) % 2, g)
                    if g < 2 and not (last and h == HEADS - 1):
                        (maximum, bias_of)[g](u + 1, (h + 1) % HEADS)
                    if g in BY_DVE:
                        copy_out(u, h, g)
                    if g == 4 and not last:
                        copy_a(i + 1, h)
                    if g in (2, 3, 5, 7) and not (first and h == 0):
                        {2: sum_up, 3: safe, 5: invert, 7: scale}[g]()
                    if h == 1 and g in (4, 5, 6) and not first:
                        (difference, logit, bound)[g - 4]()
                    if h == 3 and g in (3, 4, 5, 6) and not first:
                        (one_more, beta, scaled, finish)[g - 3]()

            for c in range(NS):
                part = slice(c * SW, (c + 1) * SW)
                dve.wait_ge(a_loaded[c], 16)
                dve.tensor_scalar(mask[:, 0, part], a_in[:, part], 0.0, HIDE, ALU.is_equal, ALU.mult).then_inc(first_mask, 1)
                copy_a(0, c, first=True)
                dve.wait_ge(first_mask, c + 1)
                for p in (2 * c, 2 * c + 1):
                    mask_part(0, 0, 0, 0, p)
            maximum(0, 0)
            bias_of(0, 0)
            for p in range(PARTS):
                mask_part(1, 1, 0, 0, p)
            for i in range(2):
                for h in range(HEADS):
                    unit(i, h, i, first=i == 0)
            with dve.Fori(1, NB // 2 - 1) as j:
                for k in range(2):
                    for h in range(HEADS):
                        unit(j * 2 + k, h, k)
            for i in (NB - 2, NB - 1):
                for h in range(HEADS):
                    unit(i, h, i % 2, last=i == NB - 1)
            for step in head_steps_of(UNITS - 1, HEADS - 1, 1) + gate_steps_of(NB - 1, 1):
                step()



def late_layers(nc, t, m, dram):
    GL = 2
    NL = NB // GL
    RING = 8
    SPLITS = 4
    LAG = 3
    with ExitStack() as ctx:
        sb = lambda name, shape, dt=F32: ctx.enter_context(nc.sbuf_tensor("ll_" + name, shape, dt))
        bank = lambda name, n=1: ctx.enter_context(nc.psum_tensor("ll_" + name, [P, n * CW], F32))
        sem = lambda name: ctx.enter_context(nc.semaphore("ll_" + name))
        x = sb("x", [P, NB, D])
        h2_group = sb("h2_group", [P, 2, CB, D])
        h2 = [sb("h2_high", [P, NB, D], F32R), sb("h2_low", [P, NB, D], F32R)]
        h3 = [sb("h3_high", [P, NB, D], F32R), sb("h3_low", [P, NB, D], F32R)]
        h_t = sb("h_t", [P, N])
        a_in = sb("a_in", [P, RING, GL, CW])
        a_high = sb("a_high", [P, SPLITS, GL, CW], F32R)
        a_low = sb("a_low", [P, SPLITS, GL, CW], F32R)
        agg = sb("agg", [P, 2, CW])
        msg, r, z, n_in, diff, new = (sb(n, [P, CW]) for n in ("msg", "r", "z", "n_in", "diff", "new"))
        x3, h_c, centred, out_c, term = (sb(n, [P, CB, D]) for n in ("x3", "h_c", "centred", "out_c", "term"))
        unused = sb("unused", [P, CB, D], BF16)
        stat = sb("stat", [P, 6, CB])
        acc = [bank(f"acc{k}") for k in range(2)]
        node, side, r_acc, z_acc, in_acc, hn_acc = (bank(n) for n in ("node", "side", "r_acc", "z_acc", "in_acc", "hn_acc"))
        first = FirstNorm(ctx, nc, "ll_first", x, lambda g: h2_group[:, g % 2])
        loaded = [sem(f"loaded{s}") for s in range(RING)]
        (high_ready, low_ready, grouped, acc_out, h2_turned, h2_out, h2_high_ready, h2_low_ready, msg_acc_ready,
         msg_ready, r_acc_ready, z_acc_ready, n_acc_ready, r_ready, z_ready, n_sum_ready, n_ready, gru_ready, gru_turned,
         mean_ready, squares_ready, var_ready, std_ready, centred_ready, x3_kept, h3_ready, h3_high_ready, h3_low_ready, sides_ready, out_ready,
         stored, steps, last_steps) = (sem(n) for n in (
             "high_ready", "low_ready", "grouped", "acc_out", "h2_turned", "h2_out", "h2_high_ready", "h2_low_ready",
             "msg_acc_ready", "msg_ready", "r_acc_ready", "z_acc_ready", "n_acc_ready", "r_ready", "z_ready",
             "n_sum_ready", "n_ready", "gru_ready", "gru_turned", "mean_ready", "squares_ready", "var_ready",
             "std_ready", "centred_ready", "x3_kept", "h3_ready", "h3_high_ready", "h3_low_ready", "sides_ready", "out_ready", "stored", "steps",
             "last_steps"))
        block = ctx.enter_context(nc.Block())
        groups = lambda v: v.rearrange("(g r p) n -> g p r n", r=GL, p=P)
        sides = (groups(dram.adj_t), groups(t["adj"]))
        x_groups = dram.x2.rearrange("(g b p) d -> g p b d", b=CB, p=P)
        out_rows = dram.out.rearrange("(c b p) d -> c p b d", b=CB, p=P)
        W_MSG, W_I, W_H = 0, 1, 4
        w = lambda k: m.w_gru[:, k, :]
        as_nodes = lambda v: v.rearrange("p (b d) -> p b d", b=CB)
        STEPS2 = 3 + NORM_STEPS
        STEPS3 = 2

        def streams(engine, body):
            body(0, 0, 0, None, None)
            body(1, 1, 1, 0, None)
            with engine.Fori(1, NCH // 2) as j:
                for k in range(2):
                    body(j * 2 + k, k, j * 2 + k, j * 2 + (k - 1), None)
            body(NCH, 0, 0, NCH - 1, None)
            body(NCH + 1, 1, 0, None, None)
            with engine.Fori(1, NCH) as c:
                body(c * 2 + NCH, 0, c, None, c - 1)
                body(c * 2 + (NCH + 1), 1, c, None, None)
            body(None, 0, None, None, NCH - 1)

        @block.sync
        def _(sp):
            def load(s, c, g, k, layer3):
                if not (isinstance(s, int) and s == 0 and g < RING):
                    wait_apart(sp, m.passed, low_ready, s * NL + g - RING + 1)
                sp.dma_start(a_in[:, g % RING], sides[k if layer3 else 0][g, :, :, bass.ts(c, CW)])\
                    .then_inc(loaded[g % RING], 16)

            def store_out(e):
                wait_apart(sp, m.passed, out_ready, e + 1)
                sp.dma_start(at(out_rows, e), out_c[:]).then_inc(stored, 16)

            def body(s, k, c, e, e3):
                if s is None:
                    return store_out(e3)
                layer3 = not isinstance(s, int) and e is None or isinstance(s, int) and s >= NCH
                for g in range(NL):
                    if isinstance(s, int) and s == 0 and g % 2 == 0:
                        gg = g // 2
                        sp.dma_start(x[:, gg * CB:(gg + 1) * CB, :], x_groups[gg]).then_inc(first.x_loaded[gg], 16)
                    load(s, c, g, k, layer3)
                    if e3 is not None and g == NL - 1:
                        store_out(e3)

            streams(sp, body)
            sp.wait_ge(stored, 16 * NCH)

        @block.tensor
        def _(pe):
            def group(s, k, g, state):
                high, low = state
                pe.wait_ge(low_ready, s * NL + g + 1)
                if g == 0 and not (isinstance(s, int) and s < 2):
                    pe.wait_ge(acc_out, s - 1)
                for b in range(GL):
                    j = g * GL + b
                    upper, rest = a_high[:, g % SPLITS, b, :], a_low[:, g % SPLITS, b, :]
                    pe.matmul(acc[k][:], high[:, j, :], upper, start=(j == 0), stop=False)
                    pe.matmul(acc[k][:], high[:, j, :], rest, start=False, stop=False)
                    last = pe.matmul(acc[k][:], low[:, j, :], upper, start=False, stop=(j == NB - 1))
                last.then_inc(grouped, 1)

            def turn(to, blocks, ready):
                for b in range(CB):
                    last = pe.transpose(to[:, b * P:(b + 1) * P], blocks[b], m.ident[:])
                last.then_inc(ready, 1)

            def gates(e):
                h_e = h_t[:, bass.ts(e, CW)]
                pe.matmul(hn_acc[:], w(W_H + 2), h_e, start=True, stop=True)
                pe.matmul(r_acc[:], w(W_H), h_e, start=True, stop=False)
                pe.matmul(z_acc[:], w(W_H + 1), h_e, start=True, stop=False)
                pe.wait_ge(msg_ready, e + 1)
                pe.matmul(r_acc[:], w(W_I), msg[:], start=False, stop=True).then_inc(r_acc_ready, 1)
                pe.matmul(in_acc[:], w(W_I + 2), msg[:], start=True, stop=True).then_inc(n_acc_ready, 1)
                pe.matmul(z_acc[:], w(W_I + 1), msg[:], start=False, stop=True).then_inc(z_acc_ready, 1)

            def project_sides(s, e3):
                if not (isinstance(e3, int) and e3 == 0):
                    pe.wait_ge(out_ready, e3)
                for k, to in enumerate((node, side)):
                    pe.wait_ge(acc_out, e3 * 2 + (NCH + 1 + k))
                    for b in range(CB):
                        last = pe.matmul(to[:, b * D:(b + 1) * D], agg[:, k, b * P:(b + 1) * P],
                                         m.w_io[:, k * D:(k + 1) * D], start=True, stop=True)
                    last.then_inc(sides_ready, 1)

            def body(s, k, c, e, e3):
                opening = isinstance(s, int) and s == 0
                layer3 = not isinstance(s, int) and e is None or isinstance(s, int) and s >= NCH
                for g in range(NL):
                    if opening and g % 2 == 0:
                        gg = g // 2
                        if gg >= 2:
                            pe.wait_ge(h2_out, gg - 1)
                        pe.wait_ge(first.h_ready, gg + 1)
                        turn((node, side)[gg % 2], [h2_group[:, gg % 2, b, :] for b in range(CB)], h2_turned)
                        pe.wait_ge(h2_low_ready, gg + 1)
                    if layer3 and e is not None and g in (0, NL - GR // GL):
                        pe.wait_ge(h3_low_ready, NCH - 1 if g == 0 else NCH)
                    if s is not None:
                        group(s, k, g, h3 if layer3 else h2)
                    if e is not None:
                        if g == 1:
                            if isinstance(e, int) and e == 0:
                                pe.wait_ge(h2_out, NG)
                            pe.wait_ge(acc_out, e + 1)
                            pe.matmul(side[:], w(W_MSG), agg[:, 0, :], start=True, stop=True).then_inc(msg_acc_ready, 1)
                        elif g == 2:
                            gates(e)
                        elif g == 7:
                            pe.wait_ge(gru_ready, e + 1)
                            turn(node, [new[:, b * P:(b + 1) * P] for b in range(CB)], gru_turned)
                    if e3 is not None and g == 2:
                        project_sides(s, e3)

            streams(pe, body)

        @block.scalar
        def _(act):
            def upper(s, g):
                act.wait_ge(loaded[g % RING], s * (16 * NL // RING) + 16 * (g // RING) + 16)
                if not (isinstance(s, int) and s == 0 and g < SPLITS):
                    act.wait_ge(grouped, s * NL + g - SPLITS + 1)
                act.activation(a_high[:, g % SPLITS], a_in[:, g % RING], ACT.Copy).then_inc(high_ready, 1)

            def copy_acc(s, k, to):
                act.wait_ge(grouped, s * NL)
                act.activation(agg[:, to, :], acc[1 - k][:], ACT.Copy).then_inc(acc_out, 1)

            def behind2(g, e):
                if g == 1:
                    act.wait_ge(msg_acc_ready, e + 1)
                    act.activation(msg[:], side[:], ACT.Relu, bias=m.b_msg[:]).then_inc(msg_ready, 1)
                elif g == 2:
                    act.wait_ge(r_acc_ready, e + 1)
                    act.activation(r[:], r_acc[:], ACT.Sigmoid, bias=m.b_rz[:, 0:1]).then_inc(r_ready, 1)
                elif g == 3:
                    act.wait_ge(z_acc_ready, e + 1)
                    act.activation(z[:], z_acc[:], ACT.Sigmoid, bias=m.b_rz[:, 1:2]).then_inc(z_ready, 1)
                elif g == 4:
                    act.wait_ge(n_sum_ready, e + 1)
                    act.activation(n_in[:], n_in[:], ACT.Tanh, bias=m.b_ih[:, 2:3]).then_inc(n_ready, 1)
                elif g == 9:
                    norm_squares(act, x3, unused, stat, CB, mean_ready, squares_ready, e + 1)
                elif g == 10:
                    norm_root(act, stat, var_ready, std_ready, e + 1)
                elif g == 12:
                    act.wait_ge(h3_ready, e + 1)
                    act.sem_inc(m.passed, 1)
                    act.activation(h3[0][:, bass.ts(e, CB), :], h_c[:], ACT.Copy).then_inc(h3_high_ready, 1)

            def body(s, k, c, e, e3):
                if s is None:
                    act.wait_ge(grouped, 3 * NCH * NL)
                    act.activation(agg[:, 1, :], acc[1][:], ACT.Copy).then_inc(acc_out, 1)
                    return
                if isinstance(s, int) and s == 0:
                    first.squares(act, 0)
                    first.root(act, 0)
                    upper(s, 0)
                    upper(s, 1)
                    for g in range(NG):
                        if g < NG - 1:
                            first.squares(act, g + 1)
                        act.wait_ge(first.h_ready, g + 1)
                        act.activation(h2[0][:, g * CB:(g + 1) * CB, :], h2_group[:, g % 2], ACT.Copy).then_inc(h2_high_ready, 1)
                        if g < NG - 1:
                            upper(s, 2 * g + 2)
                            upper(s, 2 * g + 3)
                            first.root(act, g + 1)
                        act.wait_ge(h2_turned, g + 1)
                        act.activation(h_t[:, g * CW:(g + 1) * CW], (node, side)[g % 2][:], ACT.Copy).then_inc(h2_out, 1)
                    return
                for g in range(NL):
                    upper(s, g)
                    if g == 1:
                        copy_acc(s, k, 0 if e is not None else 1 - k)
                    if e is not None and g >= LAG:
                        behind2(g - LAG, e)

            streams(act, body)

        @block.vector
        def _(dve):
            def rest(s, g):
                dve.wait_ge(high_ready, s * NL + g + 1)
                dve.tensor_tensor(a_low[:, g % SPLITS], a_in[:, g % RING], a_high[:, g % SPLITS].bitcast(F32), ALU.subtract)\
                    .then_inc(low_ready, 1)

            def behind2(g, e, step):
                if g == 3:
                    dve.wait_ge(r_ready, e + 1)
                    step(dve.scalar_tensor_tensor(n_in[:], hn_acc[:], m.b_hh[:, 2:3], r[:], ALU.add, ALU.mult))
                    dve.wait_ge(n_acc_ready, e + 1)
                    dve.tensor_tensor(n_in[:], n_in[:], in_acc[:], ALU.add).then_inc(n_sum_ready, 1)
                elif g == 5:
                    dve.wait_ge(n_ready, e + 1)
                    step(dve.tensor_tensor(diff[:], h_t[:, bass.ts(e, CW)], n_in[:], ALU.subtract))
                    dve.wait_ge(z_ready, e + 1)
                    step(dve.tensor_tensor(diff[:], diff[:], z[:], ALU.mult))
                    dve.tensor_tensor(new[:], n_in[:], diff[:], ALU.add).then_inc(gru_ready, 1)
                elif g == 8:
                    x_e = x[:, bass.ts(e, CB), :]
                    if not (isinstance(e, int) and e == 0):
                        dve.wait_ge(x3_kept, e)
                    dve.wait_ge(gru_turned, e + 1)
                    step(dve.tensor_tensor(x3[:], x_e, as_nodes(node[:]), ALU.add))
                    norm_mean(step, dve, x3[:], stat, mean_ready)
                elif g == 9:
                    norm_variance(dve, stat, squares_ready, var_ready, e + 1)
                elif g == 10:
                    dve.wait_ge(centred_ready, e + 1)
                    norm_scale(step, dve, h_c[:], centred[:], stat, CB, std_ready, e + 1).then_inc(h3_ready, 1)

            def add_sides(e):
                step = Chain(dve, last_steps, e * STEPS3)
                inverse = lambda v: over(v[:, bass.ts(e, CB)], CB)
                if not (isinstance(e, int) and e == 0):
                    dve.wait_ge(stored, e * 16)
                if isinstance(e, int) and e == 0:
                    dve.wait_ge(x3_kept, NCH)
                dve.wait_ge(sides_ready, e * 2 + 2)
                step(dve.tensor_tensor(out_c[:], as_nodes(node[:]), inverse(m.row_inv), ALU.mult))
                dve.tensor_tensor(term[:], as_nodes(side[:]), inverse(m.col_inv), ALU.mult)
                step(dve.tensor_tensor(out_c[:], out_c[:], x[:, bass.ts(e, CB), :], ALU.add))
                dve.tensor_tensor(out_c[:], out_c[:], term[:], ALU.add).then_inc(out_ready, 1)

            def body(s, k, c, e, e3):
                if s is None:
                    return add_sides(e3)
                opening = isinstance(s, int) and s == 0
                step = Chain(dve, first.steps) if opening else Chain(dve, steps, e * STEPS2) if e is not None else None
                if opening:
                    first.begin(dve, step, 0)
                    first.variance(dve, 0)
                for g in range(NL):
                    gg = g // 2
                    if opening and g % 2 == 0:
                        if gg < NG - 1:
                            first.begin(dve, step, gg + 1)
                        if gg >= 2:
                            dve.wait_ge(h2_turned, gg - 1)
                            dve.wait_ge(h2_low_ready, gg - 1)
                        first.finish(dve, step, gg)
                    rest(s, g)
                    if opening and g % 2 and gg < NG - 1:
                        first.variance(dve, gg + 1)
                    if e is not None and g >= LAG:
                        behind2(g - LAG, e, step)
                    if e3 is not None and g == 2 + LAG:
                        add_sides(e3)
                assert e is None or step.n == STEPS2, step.n

            streams(dve, body)

        @block.gpsimd
        def _(pool):
            first.centre(pool, 0)
            for g in range(NG):
                if g < NG - 1:
                    first.centre(pool, g + 1)
                rows = slice(g * CB, (g + 1) * CB)
                pool.wait_ge(h2_high_ready, g + 1)
                pool.tensor_tensor(h2[1][:, rows, :], h2_group[:, g % 2], h2[0][:, rows, :].bitcast(F32), ALU.subtract)\
                    .then_inc(h2_low_ready, 1)

            with pool.Fori(0, NCH) as e:
                rows = bass.ts(e, CB)
                wait_apart(pool, m.passed, mean_ready, e + 1)
                pool.tensor_tensor(centred[:], x3[:], over(stat[:, 1, :], CB), ALU.add).then_inc(centred_ready, 1)
                pool.tensor_copy(x[:, rows, :], x3[:]).then_inc(x3_kept, 1)
                wait_apart(pool, m.passed, h3_high_ready, e + 1)
                pool.tensor_tensor(h3[1][:, rows, :], h_c[:], h3[0][:, rows, :].bitcast(F32), ALU.subtract)\
                    .then_inc(h3_low_ready, 1)


def graph_layers(nc, t, out, phases=(layer0, attention, late_layers)):
    scratch = lambda name, shape: nc.dram_tensor(name, shape, F32, kind="Internal").ap()
    dram = Places()
    dram.adj_t, dram.out = scratch("adj_t", [N, N]), out
    dram.x1, dram.skip, dram.x2 = (scratch(name, [N, D]) for name in ("x1", "skip", "x2"))
    dram.q_parts, dram.k_parts = (scratch(name, [HEADS, 2 * HC, N]) for name in ("q_parts", "k_parts"))
    with ExitStack() as ctx:
        sb = lambda name, shape, dt=F32: ctx.enter_context(nc.sbuf_tensor(name, shape, dt))
        m = Places()
        m.ident, m.ident_sum, m.ones = sb("ident", [P, P]), sb("ident_sum", [P, HC]), sb("ones", [P, 1])
        m.w_io, m.w_gru, m.w_beta = sb("w_io", [D, 2 * D]), sb("w_gru", [D, 7, D]), sb("w_beta", [P, 3 * D])
        m.b_msg = sb("b_msg", [D, 1])
        m.b_ih, m.b_hh, m.b_rz = sb("b_ih", [D, 3]), sb("b_hh", [D, 3]), sb("b_rz", [D, 2])
        m.row_inv, m.col_inv = sb("row_inv", [P, NB]), sb("col_inv", [P, NB])
        m.passed = ctx.enter_context(nc.semaphore("passed"))
        with ExitStack() as attention_only:
            asb = lambda name, shape, dt=F32: attention_only.enter_context(nc.sbuf_tensor(name, shape, dt))
            m.k_stack = asb("k_stack_sb", [P, HEADS, N], F32R)
            m.v = asb("v", [P, NB, D])
            for phase in phases[:2]:
                phase(nc, t, m, dram)
        for phase in phases[2:]:
            phase(nc, t, m, dram)


_INS = ['x', 'adj', 'L1_gnn_Wq', 'L1_gnn_bq', 'L1_gnn_Wk', 'L1_gnn_bk', 'L1_gnn_Wv', 'L1_gnn_bv', 'L1_gnn_Ws',
        'L1_gnn_bs', 'L1_gnn_Wb', 'L2_gnn_W_msg', 'L2_gnn_b_msg', 'L2_gnn_W_ih', 'L2_gnn_W_hh', 'L2_gnn_b_ih',
        'L2_gnn_b_hh', 'L3_gnn_W_in', 'L3_gnn_W_out']


def kernel(**inputs):
    import numpy as np
    import concourse.bacc as bacc
    from concourse.bass_utils import run_bass_kernel_spmd

    nc = bacc.Bacc("TRN2", target_bir_lowering=False, num_devices=1)
    arrays, tensors = {}, {}
    for name in _INS:
        a = np.ascontiguousarray(inputs[name])
        arrays[name + "_in"] = a
        tensors[name] = nc.dram_tensor(name + "_in", a.shape, mybir.dt.from_np(a.dtype), kind="ExternalInput").ap()
    out = nc.dram_tensor("out", (N, D), F32, kind="ExternalOutput").ap()
    graph_layers(nc, tensors, out)
    return run_bass_kernel_spmd(nc, [arrays], core_ids=[0]).results[0]["out"]
```
